# Optimizing a Trainium2 kernel written in Bass

```python
import numpy as np
import jax
import jax.numpy as jnp

def _softmax(x, axis=-1):
    return jax.nn.softmax(x, axis=axis)

def _gelu(x):
    return jax.nn.gelu(x, approximate=True)

def _silu(x):
    return jax.nn.silu(x)

def _sigmoid(x):
    return jax.nn.sigmoid(x)

def _layernorm(x, axis=-1, eps=1e-05):
    m = jnp.mean(x, axis=axis, keepdims=True)
    v = jnp.var(x, axis=axis, keepdims=True)
    return (x - m) / jnp.sqrt(v + eps)

def _scatter_add(tgt, idx, src, axis=0):
    return tgt.at[idx].add(src)

def _segment_sum(src, seg, n):
    return jax.ops.segment_sum(src, seg, n)
kernel_name = 'mk_xattn_ffn_d1_seqx_r4_bd3beb'

def setup_inputs(seed: int=0):
    np.random.seed(seed)
    _w = jnp.asarray

    def _rec_inputs():
        import jax
        import jax.numpy as jnp
        _rk = jax.random.key(seed)
        x = 7.22e-05 + 1 * jax.random.normal(jax.random.fold_in(_rk, 1), (2, 512, 256), jnp.float32)
        _lenS = 512 - jax.random.randint(jax.random.fold_in(_rk, 7), (2,), 0, max(1, 512 // 4) + 1, jnp.int32)
        _lenS2 = 1024 - jax.random.randint(jax.random.fold_in(_rk, 8), (2,), 0, max(1, 1024 // 4) + 1, jnp.int32)
        _ctx_1024P = jax.random.normal(jax.random.fold_in(_rk, 11), (2, 16, 256), jnp.float32)
        _ctx_1024c = jax.random.dirichlet(jax.random.fold_in(_rk, 511), 0.3 * jnp.ones((16,), jnp.float32), (2, 1024))
        _ctx_1024t = jnp.einsum('bsk,bkd->bsd', _ctx_1024c, _ctx_1024P)
        _ctx_1024t = _ctx_1024t * jax.lax.rsqrt(jnp.mean(jnp.square(_ctx_1024t)) + 1e-12) * 0.953939
        ctx_1024 = 4.13588e-05 + 0.999923 * (_ctx_1024t + 0.3 * jax.random.normal(jax.random.fold_in(_rk, 611), (2, 1024, 256), jnp.float32))
        return (x, ctx_1024)
    x, ctx_1024 = _rec_inputs()

    def _L0_xattn_setup():
        import jax, jax.numpy as jnp
        import numpy as np
        B, S, E, H = (4, 512, 256, 16)
        D = E // H
        key = jax.random.key(seed)
        ks = jax.random.split(key, 12)
        s_in = 1.0 / np.sqrt(E)
        inp = {'query': jax.random.normal(ks[0], (B, S, E), jnp.float32), 'key': jax.random.normal(ks[1], (B, S, E), jnp.float32), 'value': jax.random.normal(ks[2], (B, S, E), jnp.float32), 'Wq': jax.random.normal(ks[3], (H, E, D), jnp.float32) * s_in, 'bq': jax.random.normal(ks[4], (H, D), jnp.float32) * s_in, 'Wk': jax.random.normal(ks[5], (H, E, D), jnp.float32) * s_in, 'bk': jax.random.normal(ks[6], (H, D), jnp.float32) * s_in, 'Wv': jax.random.normal(ks[7], (H, E, D), jnp.float32) * s_in, 'bv': jax.random.normal(ks[8], (H, D), jnp.float32) * s_in, 'Wo': jax.random.normal(ks[9], (E, E), jnp.float32) * s_in, 'bo': jax.random.normal(ks[10], (E,), jnp.float32) * s_in}
        return inp
    _L0_xattn_all = _L0_xattn_setup()
    _L0_xattn_in = {k: v for k, v in _L0_xattn_all.items() if k in ('Wq', 'bq', 'Wk', 'bk', 'Wv', 'bv', 'Wo', 'bo')}
    del _L0_xattn_all

    def _L0_ffn_setup():
        import math
        import jax, jax.numpy as jnp
        import numpy as np
        TOP_K = 2
        _GELU_C = math.sqrt(2.0 / math.pi)

        def gelu_new(x):
            return 0.5 * x * (1.0 + jnp.tanh(_GELU_C * (x + 0.044715 * x * x * x)))
        key = jax.random.key(seed)
        ks = jax.random.split(key, 6)
        B, T, C, E, H = (2, 512, 256, 8, 1024)
        s_in = 1.0 / math.sqrt(C)
        s_hid = 1.0 / math.sqrt(H)
        return {'x': jax.random.normal(ks[0], (B, T, C), dtype=jnp.float32), 'router_w': jax.random.normal(ks[1], (E, C), dtype=jnp.float32) * s_in, 'w_fc': jax.random.normal(ks[2], (E, C, H), dtype=jnp.float32) * s_in, 'b_fc': jax.random.normal(ks[3], (E, H), dtype=jnp.float32) * 0.02, 'w_proj': jax.random.normal(ks[4], (E, H, C), dtype=jnp.float32) * s_hid, 'b_proj': jax.random.normal(ks[5], (E, C), dtype=jnp.float32) * 0.02}
    _L0_ffn_all = _L0_ffn_setup()
    _L0_ffn_in = {k: v for k, v in _L0_ffn_all.items() if k in ('router_w', 'w_fc', 'b_fc', 'w_proj', 'b_proj')}
    del _L0_ffn_all
    return {'x': x, 'ctx_1024': ctx_1024, 'L0_xattn_Wq': _L0_xattn_in['Wq'], 'L0_xattn_bq': _L0_xattn_in['bq'], 'L0_xattn_Wk': _L0_xattn_in['Wk'], 'L0_xattn_bk': _L0_xattn_in['bk'], 'L0_xattn_Wv': _L0_xattn_in['Wv'], 'L0_xattn_bv': _L0_xattn_in['bv'], 'L0_xattn_Wo': _L0_xattn_in['Wo'], 'L0_xattn_bo': _L0_xattn_in['bo'], 'L0_ffn_router_w': _L0_ffn_in['router_w'], 'L0_ffn_w_fc': _L0_ffn_in['w_fc'], 'L0_ffn_b_fc': _L0_ffn_in['b_fc'], 'L0_ffn_w_proj': _L0_ffn_in['w_proj'], 'L0_ffn_b_proj': _L0_ffn_in['b_proj']}

def reference(x, ctx_1024, L0_xattn_Wq, L0_xattn_bq, L0_xattn_Wk, L0_xattn_bk, L0_xattn_Wv, L0_xattn_bv, L0_xattn_Wo, L0_xattn_bo, L0_ffn_router_w, L0_ffn_w_fc, L0_ffn_b_fc, L0_ffn_w_proj, L0_ffn_b_proj):
    import jax
    import jax.numpy as jnp

    def _L0_xattn_ref(query, key, value, Wq, bq, Wk, bk, Wv, bv, Wo, bo):
        import jax, jax.numpy as jnp
        import numpy as np
        B, S, E, H = (4, 512, 256, 16)
        D = E // H
        q = jnp.einsum('bse,hed->bhsd', query, Wq) + bq[None, :, None, :]
        k = jnp.einsum('bse,hed->bhsd', key, Wk) + bk[None, :, None, :]
        v = jnp.einsum('bse,hed->bhsd', value, Wv) + bv[None, :, None, :]
        scale = 1.0 / jnp.sqrt(jnp.asarray(D, q.dtype))
        scores = jnp.einsum('bhsd,bhtd->bhst', q, k) * scale
        weights = jax.nn.softmax(scores, axis=-1)
        attn = jnp.einsum('bhst,bhtd->bhsd', weights, v)
        x = attn.transpose(0, 2, 1, 3).reshape(query.shape[0], query.shape[1], -1)
        return x @ Wo + bo

    def _L0_ffn_ref(x, router_w, w_fc, b_fc, w_proj, b_proj):
        import math
        import jax, jax.numpy as jnp
        import numpy as np
        TOP_K = 2
        _GELU_C = math.sqrt(2.0 / math.pi)

        def gelu_new(x):
            return 0.5 * x * (1.0 + jnp.tanh(_GELU_C * (x + 0.044715 * x * x * x)))
        B, T, C = x.shape
        E = router_w.shape[0]
        N = B * T
        xf = x.reshape(N, C)
        logits = xf @ router_w.T
        probs = jax.nn.softmax(logits, axis=-1)
        topk_probs, topk_idx = jax.lax.top_k(probs, TOP_K)
        topk_probs = topk_probs / jnp.sum(topk_probs, axis=-1, keepdims=True)
        combine = jnp.zeros((N, E), dtype=x.dtype).at[jnp.arange(N)[:, None], topk_idx].add(topk_probs)
        h = gelu_new(jnp.einsum('nc,ech->neh', xf, w_fc) + b_fc)
        out = jnp.einsum('neh,ehc->nec', h, w_proj) + b_proj
        y = jnp.einsum('nec,ne->nc', out, combine)
        return y.reshape(B, T, C)
    x = x + _L0_xattn_ref(_layernorm(x, axis=-1), ctx_1024, ctx_1024, L0_xattn_Wq, L0_xattn_bq, L0_xattn_Wk, L0_xattn_bk, L0_xattn_Wv, L0_xattn_bv, L0_xattn_Wo, L0_xattn_bo)
    x = x + _L0_ffn_ref(_layernorm(x, axis=-1), L0_ffn_router_w, L0_ffn_w_fc, L0_ffn_b_fc, L0_ffn_w_proj, L0_ffn_b_proj)
    return x

_drawn_inputs = setup_inputs


def setup_inputs(seed=0):
    import zlib

    import numpy as np

    out = dict(_drawn_inputs(seed))
    spreads = {}
    factors = {'L0_xattn_bk': 8.0, 'L0_ffn_b_fc': 6.806, 'L0_ffn_b_proj': 4.464}
    for name, (base, spread) in spreads.items():
        noise = np.random.default_rng([zlib.crc32(name.encode()), seed]).standard_normal(out[name].shape)
        drawn = base * np.exp(spread * noise) if base else spread * noise
        out[name] = jnp.asarray(drawn.astype(out[name].dtype))
    for name, factor in factors.items():
        out[name] = (out[name] * factor).astype(out[name].dtype)
    return out
```

```python
from contextlib import ExitStack

import numpy as np

import concourse.bass as bass
from concourse import mybir

F32 = mybir.dt.float32
BF16 = mybir.dt.bfloat16
U32 = mybir.dt.uint32
ALU = mybir.AluOpType
ACT = mybir.ActivationFunctionType
AX_X = mybir.AxisListType.X

P = 128
BANK = 512
EPS = 1e-5
PART_PAIRS = [(0, 0), (0, 1), (0, 2), (1, 0), (1, 1), (2, 0)]


class Lane:

    def __init__(self, sem):
        self.sem = sem
        self.count = 0
        self.program = []
        self.passed = {}

    def do(self, fn):
        self.program.append(fn)

    def done(self, fn):
        self.count += 1
        self.program.append(lambda e: fn(e).then_inc(self.sem, 1))
        return (self.sem, self.count)

    def dma(self, fn, sem):
        sem.count += 16
        self.program.append(lambda e: fn(e).then_inc(sem.sem, 16))
        return (sem.sem, sem.count)

    def wait(self, *tokens):
        for sem, value in tokens:
            if self.passed.get(id(sem), 0) < value:
                self.passed[id(sem)] = value
                self.program.append(lambda e, s=sem, v=value: e.wait_ge(s, v))

    def step(self, fn):
        token = self.done(fn)
        self.wait(token)
        return token

    def emit(self, engine):
        for fn in self.program:
            fn(engine)


class DmaCount:
    def __init__(self, sem):
        self.sem = sem
        self.count = 0


def xattn_moe_block(nc, x, ctx_t, wq, bq, wk, bk, wv, bv, wo, bo, router_t, w_fc, b_fc, w_proj, b_proj, out):
    N, E = x.shape
    T = ctx_t.shape[1]
    B = 2
    S, TB = N // B, T // B
    H, D = 16, 16
    NE, _, HID = w_fc.shape
    EC = E // P
    NT = N // P
    TT = T // P
    ST = S // P
    KT = TB // P
    HG = 4
    NG = H // HG
    HPM = P // D
    NPART = 3
    STACK = D * len(PART_PAIRS)
    HC = HID // P
    SCALE = 1.0 / np.sqrt(D)

    ctx = ExitStack()
    with ctx:
        def sb(name, shape, dt=F32):
            return ctx.enter_context(nc.sbuf_tensor(name, shape, dt))

        def sem(name):
            return ctx.enter_context(nc.semaphore(name))

        x_sb = sb("x_sb", [P, NT, E])
        xn = sb("xn", [P, NT, E])
        xT = sb("xT", [P, EC, N])
        ctx_p = sb("ctx_p", [P, EC * T])
        ctxT = ctx_p[:, :].rearrange("p (c t) -> p c t", c=EC)
        prob = ctx_p[:, :].rearrange("p (r h s) -> p r h s", r=2, h=HG)
        wq_sb, wk_sb, wv_sb, wo_sb = (sb(n, [P, EC, E]) for n in ("wq_sb", "wk_sb", "wv_sb", "wo_sb"))
        bq_sb, bk_sb = sb("bq_sb", [P, EC]), sb("bk_sb", [P, EC])
        bv_sb, bo_sb = sb("bv_sb", [P, E]), sb("bo_sb", [P, E])
        k_stack = sb("k_stack", [P, B, H, TB], BF16)
        q_stack = sb("q_stack", [P, H, N], BF16)
        v_ones = sb("v_ones", [P, TT, H, 2 * D])
        parts = sb("parts", [P, 2, NPART, 1024], BF16)
        rest = sb("rest", [P, 2, 1024])
        ident = sb("ident", [P, P])
        ident_b = sb("ident_b", [P, P], BF16)
        eps_sb = sb("eps_sb", [P, 1])
        stats = sb("stats", [P, NT, 6])
        mv = sb("mv", [P, NT, 2])
        rstd = sb("rstd", [P, NT])
        mx_half = sb("mx_half", [P, 2, HG * ST, 2])
        neg_f = sb("neg_f", [P, 2, HG * ST])
        neg_p = sb("neg_p", [P, ST, NPART, HG], BF16)
        negT = sb("negT", [NPART * HG, 2, S], BF16)
        oT = sb("oT", [P, S])
        rsum = sb("rsum", [P, ST * HG])
        k0 = k_stack[:, 0, :, :].rearrange("p h t -> p (h t)").bitcast(F32)
        half = EC * HID
        w_fc_sb = [k0[:, r * 2 * half:r * 2 * half + half].rearrange("p (c h) -> p c h", c=EC) for r in range(2)]
        w_pr_sb = [k0[:, r * 2 * half + half:(r + 1) * 2 * half].rearrange("p (c n) -> p c n", c=HC) for r in range(2)]
        vflat = v_ones[:, :, :, :].rearrange("p t h d -> p (t h d)")
        hidT = [vflat[:, r * HC * S:(r + 1) * HC * S].rearrange("p (c s) -> p c s", c=HC) for r in range(2)]
        b_fc_sb = sb("b_fc_sb", [P, NE, HC])
        b_pr_sb = sb("b_pr_sb", [NE, E])
        router_sb = sb("router_sb", [P, EC, NE])
        logit = sb("logit", [P, NT, NE])
        gate = sb("gate", [P, NT, NE])
        red = sb("red", [P, NT])
        top8 = sb("top8", [P, NT, 8])
        idx8 = sb("idx8", [P, NT, 8], U32)
        idxf = sb("idxf", [P, NT, 2])
        iota_e = sb("iota_e", [P, NE])
        hot = sb("hot", [P, 2, NT, NE])
        comb = sb("comb", [P, NT, NE])
        combT = rest[0:NE, 0, :]

        ps = ctx.enter_context(nc.psum_tensor("ps", [P, 8, BANK], F32))
        ST_BANKS, MAX_BANKS, O_BANK, MISC = 0, 4, 6, 7

        pe, dve, act, pool, sp = (Lane(sem("s_" + n)) for n in ("pe", "dve", "act", "pool", "sp"))

        def dsem(name):
            return DmaCount(sem(name))

        d_x, d_wk, d_wq, d_wv, d_misc, d_out = (dsem(n) for n in ("d_x", "d_wk", "d_wq", "d_wv", "d_misc", "d_out"))
        d_ctx = [dsem(f"d_ctx{b}") for b in range(B)]
        cv = ctx_t.rearrange("(c p) t -> p c t", p=P)

        def w2(w):
            return w.rearrange("(c p) n -> p c n", p=P)

        got_wk = [sp.dma(lambda e: e.dma_start(wk_sb[:, :, :], w2(wk)), d_wk),
                  sp.dma(lambda e: e.dma_start(bk_sb[:, :], bk), d_wk)][-1]
        got_ctx = [sp.dma(lambda e: e.dma_start(ctxT[:, :, 0:TB], cv[:, :, 0:TB]), d_ctx[0])]
        got_x = act.dma(lambda e: e.dma_start(x_sb[:, :, :], x.rearrange("(i p) e -> p i e", p=P)), d_x)
        got_wq = [act.dma(lambda e: e.dma_start(wq_sb[:, :, :], w2(wq)), d_wq),
                  act.dma(lambda e: e.dma_start(bq_sb[:, :], bq), d_wq)][-1]
        got_ctx.append(sp.dma(lambda e: e.dma_start(ctxT[:, :, TB:T], cv[:, :, TB:T]), d_ctx[1]))
        got_wv = sp.dma(lambda e: e.dma_start(wv_sb[:, :, :], w2(wv)), d_wv)
        for dst, src in ((wo_sb[:, :, :], w2(wo)),
                         (bv_sb[:, :], bv.partition_broadcast(P)), (bo_sb[:, :], bo.partition_broadcast(P)),
                         (router_sb[:, :, :], w2(router_t)), (b_pr_sb[:, :], b_proj),
                         (b_fc_sb[:, :, :], b_fc)):
            got_misc = sp.dma(lambda e, d=dst, s=src: e.dma_start(d, s), d_misc)

        pool.step(lambda e: e.memset(eps_sb[:, :], EPS))
        for m in (ident, ident_b):
            pool.step(lambda e, m=m: e.memset(m[:, :], 0.0))
            made_ident = pool.step(lambda e, m=m: e.affine_select(
                out=m[:, :], in_=m[:, :], compare_op=ALU.not_equal, fill=1.0, base=0,
                pattern=[[-1, P]], channel_multiplier=1))
        pair_of_ones = float(np.array([0x3F803F80], np.uint32).view(np.float32)[0])
        made_key_ones = pool.step(lambda e: e.memset(
            k_stack[STACK:STACK + NPART, :, :, :].rearrange("p b h t -> p (b h t)").bitcast(F32), pair_of_ones))
        made_v_ones = pool.step(lambda e: e.memset(v_ones[:, :, :, D:2 * D], 1.0))
        for k in range(NE):
            made_consts = pool.step(lambda e, k=k: e.memset(iota_e[:, k:k + 1], float(k)))

        def layernorm(src, ready):
            for i in range(NT):
                dve.wait(*ready[i])
                dve.step(lambda e, i=i: e.bn_stats(stats[:, i, :], src[:, i, :]))
                last = dve.done(lambda e, i=i: e.bn_aggr(mv[:, i, :], stats[:, i, :]))
            act.wait(last, made_ident)
            std = act.done(lambda e: e.activation(rstd[:, :], mv[:, :, 1], ACT.Sqrt, bias=eps_sb[:, :]))
            dve.wait(std)
            dve.step(lambda e: e.reciprocal(rstd[:, :], rstd[:, :]))
            return [dve.done(lambda e, i=i: e.tensor_scalar(
                xn[:, i, :], src[:, i, :], mv[:, i, 0:1], rstd[:, i:i + 1], ALU.subtract, ALU.mult))
                for i in range(NT)]

        normed = layernorm(x_sb, [[got_x]] * NT)

        def transpose_rows(src, dst, ready, banks, free):
            made = []
            for n in range(N // BANK):
                for c in range(EC):
                    bank = banks[(n * EC + c) % len(banks)]
                    pe.wait(*free.get(bank, []), made_ident)
                    for j in range(BANK // P):
                        i = n * (BANK // P) + j
                        pe.wait(ready[i])
                        last = pe.done(lambda e, bank=bank, j=j, i=i, c=c: e.transpose(
                            ps[:, bank, j * P:(j + 1) * P], src[:, i, c * P:(c + 1) * P], ident[:, :]))
                    eng = act if c else dve
                    eng.wait(last)
                    if c:
                        t = act.done(lambda e, bank=bank, n=n, c=c: e.activation(
                            dst[:, c, n * BANK:(n + 1) * BANK], ps[:, bank, :], ACT.Copy))
                    else:
                        t = dve.done(lambda e, bank=bank, n=n, c=c: e.tensor_copy(
                            dst[:, c, n * BANK:(n + 1) * BANK], ps[:, bank, :]))
                    free[bank] = [t]
                    made.append(t)
            return made

        free = {}
        d_parts = [dsem("d_parts0"), dsem("d_parts1")]
        parts_read = [None, None]
        blocks = 0

        def project(w, bias, src, cols, m, ready, stack_rows, which):
            nonlocal blocks
            r = blocks % 2
            b0 = 2 * r
            blocks += 1
            pe.wait(*ready, *free.get(b0, []), *free.get(b0 + 1, []))
            for n in range(2):
                for c in range(EC):
                    last = pe.done(lambda e, n=n, c=c: e.matmul(
                        ps[:, b0 + n, :], w[:, c, m * P:(m + 1) * P],
                        src[:, c, cols + n * BANK:cols + (n + 1) * BANK], start=c == 0, stop=c == EC - 1))
            block = ps[:, b0:b0 + 2, :].rearrange("p a b -> p (a b)")
            act.wait(last)
            if parts_read[r]:
                act.wait(parts_read[r])
            p1 = act.done(lambda e: e.activation(parts[:, r, 0, :], block, ACT.Identity, bias=bias[:, m:m + 1]))
            dve.wait(p1)
            left = dve.step(lambda e: e.scalar_tensor_tensor(
                rest[:, r, :], block, bias[:, m:m + 1], parts[:, r, 0, :], ALU.add, ALU.subtract))
            free[b0] = free[b0 + 1] = [left]
            act.wait(left)
            p2 = act.done(lambda e: e.activation(parts[:, r, 1, :], rest[:, r, :], ACT.Copy))
            dve.wait(p2)
            p3 = dve.done(lambda e: e.tensor_tensor(
                parts[:, r, 2, :], rest[:, r, :], parts[:, r, 1, :], ALU.subtract))
            sp.wait(p1, p2, p3)
            for hh in range(HPM):
                for g, pair in enumerate(PART_PAIRS):
                    t = sp.dma(lambda e, hh=hh, g=g, part=pair[which]: e.dma_start(
                        stack_rows(g, m * HPM + hh), parts[D * hh:D * (hh + 1), r, part, :]), d_parts[r])
            parts_read[r] = t
            return t

        k_ready, q_ready = {}, {}

        def k_block(b, m):
            k_ready[b, m] = project(wk_sb, bk_sb, ctxT, b * TB, m, [got_wk, got_ctx[b]],
                                    lambda g, h: k_stack[D * g:D * (g + 1), b, h, :], 1)

        def q_block(m):
            q_ready[m] = project(wq_sb, bq_sb, xT, 0, m, [got_wq] + xT_made,
                                 lambda g, h: q_stack[D * g:D * (g + 1), h, :], 0)

        act.wait(got_wk)
        k_block(0, 0)
        xT_made = transpose_rows(xn, xT, normed, [4, 5, 6, 7], free)
        act.wait(got_wq)
        q_block(0)
        k_block(0, 1)
        q_block(1)
        k_block(1, 0)
        k_block(1, 1)

        pe.wait(got_wv)
        for t in range(TT):
            bank = 6 + t % 2
            pe.wait(*free.get(bank, []))
            for c in range(EC):
                last = pe.done(lambda e, t=t, c=c, bank=bank: e.matmul(
                    ps[:, bank, 0:E], ctxT[:, c, t * P:(t + 1) * P], wv_sb[:, c, :], start=c == 0, stop=c == EC - 1))
            act.wait(last)
            v_made = act.done(lambda e, t=t, bank=bank: e.activation(
                v_ones[:, t, :, 0:D], ps[:, bank, 0:E].rearrange("p (h d) -> p h d", h=H), ACT.Copy))
            free[bank] = [v_made]

        groups = B * NG
        units = [(g, hh, i, n) for g in range(groups) for hh in range(HG) for i in range(ST) for n in range(TB // BANK)]
        per_group = len(units) // groups
        per_step = per_group // KT
        LEAD = per_group + per_group // 2
        emitted = 0
        max_read = [free.get(MAX_BANKS, []), free.get(MAX_BANKS + 1, [])]
        neg_made, negT_ready = {}, {}
        d_neg = [dsem("d_neg0"), dsem("d_neg1")]
        misc_read = free.get(MISC, [])

        def heads(g):
            return [HG * (g % NG) + hh for hh in range(HG)]

        def max_unit():
            nonlocal emitted
            g, hh, i, n = units[emitted]
            b, h = g // NG, heads(g)[hh]
            s = emitted % 2
            bank = MAX_BANKS + s
            pe.wait(k_ready[b, h // HPM], q_ready[h // HPM], *max_read[s])
            q0 = b * S + i * P
            made = pe.done(lambda e: e.matmul(ps[:, bank, :], q_stack[0:STACK, h, q0:q0 + P],
                                              k_stack[0:STACK, b, h, n * BANK:(n + 1) * BANK], start=True, stop=True))
            dve.wait(made)
            t = dve.done(lambda e: e.tensor_reduce(mx_half[:, g % 2, hh * ST + i, n:n + 1], ps[:, bank, :],
                                                   AX_X, ALU.max))
            max_read[s] = [t]
            emitted += 1
            if emitted % per_group == 0:
                negate(g, t)

        def negate(g, last_max):
            r = g % 2
            nf = neg_f[:, r, :]
            dve.wait(last_max)
            dve.step(lambda e: e.tensor_reduce(nf, mx_half[:, r, :, :], AX_X, ALU.max, negate=True))
            if g >= 1:
                dve.wait(neg_transposed[g - 1])
            for part in range(NPART):
                view = neg_p[:, :, part, :].rearrange("p i h -> p h i")
                src = nf.rearrange("p (h i) -> p h i", h=HG)
                t = dve.step(lambda e, v=view, s=src: e.tensor_copy(v, s))
                if part < NPART - 1:
                    dve.step(lambda e, v=view, s=src: e.tensor_tensor(s, s, v, ALU.subtract))
            neg_made[g] = t

        neg_transposed = {}

        def spread_max(g):
            nonlocal misc_read
            r = g % 2
            bankT = ps[0:NPART * HG, MISC, 0:S // 2].bitcast(BF16)
            pe.wait(neg_made[g], made_ident, *misc_read)
            for i in range(ST):
                t = pe.done(lambda e, i=i: e.transpose(
                    bankT[:, i * P:(i + 1) * P], neg_p[:, i, :, :].rearrange("p a h -> p (a h)"), ident_b[:, :]))
            neg_transposed[g] = t
            act.wait(t)
            if g >= 2:
                act.wait(negT_ready[g - 2])
            moved = act.done(lambda e: e.activation(negT[:, r, :], bankT, ACT.Copy))
            misc_read = [moved]
            sp.wait(moved)
            b = g // NG
            for hh, h in enumerate(heads(g)):
                negT_ready[g] = sp.dma(lambda e, hh=hh, h=h: e.dma_start(
                    q_stack[STACK:STACK + NPART, h, b * S:(b + 1) * S], negT[hh:NPART * HG:HG, r, :]), d_neg[r])

        exp_done = {}
        pv_done = {}
        st_read = [free.get(0, []) + free.get(1, []), free.get(2, []) + free.get(3, [])]

        def score_pair(g, j, u):
            b = g // NG
            step = g * KT + j
            pe.wait(made_key_ones, negT_ready[g], *st_read[u])
            for a in range(2):
                h = heads(g)[2 * u + a]
                made = pe.done(lambda e, a=a, h=h: e.matmul(
                    ps[:, ST_BANKS + 2 * u + a, :], k_stack[0:STACK + NPART, b, h, j * P:(j + 1) * P],
                    q_stack[0:STACK + NPART, h, b * S:(b + 1) * S], start=True, stop=True))
            act.wait(made)
            if step >= 2:
                act.wait(pv_done[step - 2])
            t = act.done(lambda e: e.activation(
                prob[:, step % 2, 2 * u:2 * u + 2, :], ps[:, ST_BANKS + 2 * u:ST_BANKS + 2 * u + 2, :],
                ACT.Exp, scale=float(SCALE)))
            st_read[u] = [t]
            exp_done[step, u] = t

        o_read = free.get(O_BANK, [])

        def weighted_values(step):
            nonlocal o_read
            g, j = step // KT, step % KT
            b = g // NG
            pe.wait(v_made, made_v_ones, exp_done[step, 0], exp_done[step, 1])
            if j == 0:
                pe.wait(*o_read)
            for hh, h in enumerate(heads(g)):
                t = pe.done(lambda e, hh=hh, h=h: e.matmul(
                    ps[2 * D * hh:2 * D * (hh + 1), O_BANK, :], v_ones[:, b * KT + j, h, :],
                    prob[:, step % 2, hh, :], start=j == 0, stop=j == KT - 1))
            pv_done[step] = t
            if j == KT - 1:
                act.wait(t)
                if g >= 1:
                    act.wait(oT_read[g - 1])
                o_moved[g] = act.done(lambda e: e.activation(oT[:, :], ps[:, O_BANK, :], ACT.Copy))
                o_read = [o_moved[g]]

        oT_read, o_moved, attn_made = {}, {}, {}

        def normalise(g):
            nonlocal misc_read
            b = g // NG
            pe.wait(o_moved[g], *misc_read)
            for i in range(ST):
                t = pe.done(lambda e, i=i: e.transpose(
                    ps[:, MISC, i * P:(i + 1) * P], oT[:, i * P:(i + 1) * P], ident[:, :]))
            oT_read[g] = t
            rows = ps[:, MISC, :].rearrange("p (i h d) -> p i h d", i=ST, h=HG)
            h0 = HG * (g % NG) * D
            dst = xn[:, b * ST:(b + 1) * ST, h0:h0 + HG * D].rearrange("p i (h d) -> p i h d", h=HG)
            rs = rsum[:, :].rearrange("p (i h) -> p i h", i=ST)
            dve.wait(t)
            dve.step(lambda e: e.reciprocal(rs, rows[:, :, :, D]))
            for i in range(ST):
                a = dve.done(lambda e, i=i: e.tensor_tensor(
                    dst[:, i, :, :], rows[:, i, :, 0:D],
                    rs[:, i, :].unsqueeze(2).to_broadcast([P, HG, D]), ALU.mult))
            attn_made[g] = a
            misc_read = [a]

        for _ in range(LEAD):
            max_unit()
            if emitted == per_group + 4:
                spread_max(0)
        for step in range(groups * KT):
            g, j = step // KT, step % KT
            score_pair(g, j, 0)
            for k in range(per_step):
                if k == per_step // 2:
                    score_pair(g, j, 1)
                if emitted < len(units):
                    max_unit()
            if step >= 1:
                weighted_values(step - 1)
            if j == 2 and g >= 1:
                normalise(g - 1)
            if j == 5 and g + 1 < groups:
                spread_max(g + 1)
        weighted_values(groups * KT - 1)
        normalise(groups - 1)

        pool.wait(got_misc, got_x, normed[-1])
        x_bo = None
        for i in range(NT):
            x_bo = pool.step(lambda e, i=i: e.tensor_tensor(x_sb[:, i, :], x_sb[:, i, :], bo_sb[:, :], ALU.add))
        dve.wait(attn_made[groups - 1], got_misc)
        attn_bv = [dve.done(lambda e, i=i: e.tensor_tensor(xn[:, i, :], xn[:, i, :], bv_sb[:, :], ALU.add))
                   for i in range(NT)]
        free = {ST_BANKS: st_read[0], ST_BANKS + 1: st_read[0], ST_BANKS + 2: st_read[1], ST_BANKS + 3: st_read[1],
                MAX_BANKS: max_read[0], MAX_BANKS + 1: max_read[1], O_BANK: o_read, MISC: misc_read}
        attnT_made = transpose_rows(xn, xT, attn_bv, [0, 1, 2, 3], free)
        x1_made = []
        for i in range(NT):
            bank = 4 + i % 4
            pe.wait(*free[bank], *attnT_made)
            for c in range(EC):
                last = pe.done(lambda e, i=i, c=c, bank=bank: e.matmul(
                    ps[:, bank, 0:E], xT[:, c, i * P:(i + 1) * P], wo_sb[:, c, :], start=c == 0, stop=c == EC - 1))
            dve.wait(last, x_bo)
            t = dve.done(lambda e, i=i, bank=bank: e.tensor_tensor(
                x_sb[:, i, :], ps[:, bank, 0:E], x_sb[:, i, :], ALU.add))
            free[bank] = [t]
            x1_made.append(t)

        h2_made = layernorm(x_sb, [[t] for t in x1_made])
        h2T_made = transpose_rows(xn, xT, h2_made, [0, 1, 2, 3], free)
        pe.wait(*h2T_made, *free[4], got_misc)
        for i in range(NT):
            for c in range(EC):
                last = pe.done(lambda e, i=i, c=c: e.matmul(
                    ps[:, 4, i * NE:(i + 1) * NE], xT[:, c, i * P:(i + 1) * P], router_sb[:, c, :],
                    start=c == 0, stop=c == EC - 1))
        lg = ps[:, 4, 0:NT * NE].rearrange("p (i e) -> p i e", i=NT)

        def over_experts(t):
            return t.unsqueeze(2).to_broadcast([P, NT, NE])

        dve.wait(last, made_consts)
        dve.step(lambda e: e.tensor_reduce(red[:, :], lg, AX_X, ALU.max))
        t = dve.step(lambda e: e.tensor_tensor(logit[:, :, :], lg, over_experts(red[:, :]), ALU.subtract))
        free[4] = [t]
        act.wait(t)
        t = act.done(lambda e: e.activation(gate[:, :, :], logit[:, :, :], ACT.Exp))
        dve.wait(t)
        dve.step(lambda e: e.tensor_reduce(red[:, :], gate[:, :, :], AX_X, ALU.add))
        dve.step(lambda e: e.reciprocal(red[:, :], red[:, :]))
        dve.step(lambda e: e.tensor_tensor(gate[:, :, :], gate[:, :, :], over_experts(red[:, :]), ALU.mult))
        for i in range(NT):
            dve.step(lambda e, i=i: e.max(top8[:, i, :], gate[:, i, :]))
            dve.step(lambda e, i=i: e.max_index(idx8[:, i, :], top8[:, i, :], gate[:, i, :]))
        dve.step(lambda e: e.tensor_copy(idxf[:, :, :], idx8[:, :, 0:2]))
        dve.step(lambda e: e.tensor_tensor(red[:, :], top8[:, :, 0], top8[:, :, 1], ALU.add))
        dve.step(lambda e: e.reciprocal(red[:, :], red[:, :]))
        dve.step(lambda e: e.tensor_tensor(top8[:, :, 0:2], top8[:, :, 0:2],
                                           red[:, :].unsqueeze(2).to_broadcast([P, NT, 2]), ALU.mult))
        for a in range(2):
            dve.step(lambda e, a=a: e.tensor_tensor(hot[:, a, :, :], iota_e[:, :].unsqueeze(1).to_broadcast([P, NT, NE]),
                                                    over_experts(idxf[:, :, a]), ALU.is_equal))
            dve.step(lambda e, a=a: e.tensor_tensor(hot[:, a, :, :], hot[:, a, :, :],
                                                    over_experts(top8[:, :, a]), ALU.mult))
        comb_made = dve.step(lambda e: e.tensor_tensor(comb[:, :, :], hot[:, 0, :, :], hot[:, 1, :, :], ALU.add))

        for n in range(2):
            bank = 5 + n
            pe.wait(comb_made, *free[bank])
            for j in range(4):
                last = pe.done(lambda e, j=j, n=n, bank=bank: e.transpose(
                    ps[0:NE, bank, j * P:(j + 1) * P], comb[:, 4 * n + j, :], ident[:, :]))
            act.wait(last)
            t = act.done(lambda e, n=n, bank=bank: e.activation(
                combT[:, n * BANK:(n + 1) * BANK], ps[0:NE, bank, :], ACT.Copy))
            free[bank] = [t]
            pe.wait(t)
        y_made = [None] * NT
        for i in range(NT):
            bank = 4 + i % 4
            pe.wait(*free[bank])
            last = pe.done(lambda e, i=i, bank=bank: e.matmul(
                ps[:, bank, 0:E], combT[:, i * P:(i + 1) * P], b_pr_sb[:, :], start=True, stop=True))
            dve.wait(last)
            y_made[i] = dve.done(lambda e, i=i, bank=bank: e.tensor_tensor(
                x_sb[:, i, :], ps[:, bank, 0:E], x_sb[:, i, :], ALU.add))
            free[bank] = [y_made[i]]

        d_w = [dsem("d_w0"), dsem("d_w1")]
        w_used = {}
        k0_free = pv_done[NG * KT - 1]
        hid_read = {0: pv_done[groups * KT - 1], 1: pv_done[groups * KT - 1]}
        turn = 0
        for x_ in range(NE):
            r = x_ % 2
            if x_ >= 2:
                sp.wait(w_used[x_ - 2])
            else:
                sp.wait(k0_free)
            sp.dma(lambda e, x_=x_, r=r: e.dma_start(w_fc_sb[r], w_fc[x_].rearrange("(c p) h -> p c h", p=P)), d_w[r])
            w_got = sp.dma(lambda e, x_=x_, r=r: e.dma_start(
                w_pr_sb[r], w_proj[x_].rearrange("(c p) n -> p c n", p=P)), d_w[r])
            for n in range(N // BANK):
                hb = turn % 2
                turn += 1
                for c2 in range(HC):
                    bank = c2 % 4
                    pe.wait(w_got, *free[bank])
                    for c in range(EC):
                        last = pe.done(lambda e, r=r, c=c, c2=c2, n=n, bank=bank: e.matmul(
                            ps[:, bank, :], w_fc_sb[r][:, c, c2 * P:(c2 + 1) * P],
                            xT[:, c, n * BANK:(n + 1) * BANK], start=c == 0, stop=c == EC - 1))
                    act.wait(last, hid_read[hb])
                    t = act.done(lambda e, x_=x_, c2=c2, hb=hb, bank=bank: e.activation(
                        hidT[hb][:, c2, :], ps[:, bank, :], ACT.Gelu_apprx_tanh, bias=b_fc_sb[:, x_, c2:c2 + 1]))
                    free[bank] = [t]
                hid_made = t
                for j in range(BANK // P):
                    i = n * (BANK // P) + j
                    bank = 4 + j
                    pe.wait(hid_made, *free[bank])
                    for c2 in range(HC):
                        last = pe.done(lambda e, r=r, c2=c2, j=j, hb=hb, bank=bank: e.matmul(
                            ps[:, bank, 0:E], hidT[hb][:, c2, j * P:(j + 1) * P], w_pr_sb[r][:, c2, :],
                            start=c2 == 0, stop=c2 == HC - 1))
                    dve.wait(last, y_made[i])
                    y_made[i] = dve.done(lambda e, i=i, x_=x_, bank=bank: e.scalar_tensor_tensor(
                        x_sb[:, i, :], ps[:, bank, 0:E], comb[:, i, x_:x_ + 1], x_sb[:, i, :], ALU.mult, ALU.add))
                    free[bank] = [y_made[i]]
                hid_read[hb] = last
            w_used[x_] = last
        for i in range(NT):
            sp.wait(y_made[i])
            all_out = sp.dma(lambda e, i=i: e.dma_start(out[i * P:(i + 1) * P, :], x_sb[:, i, :]), d_out)
        sp.wait(all_out)

        block = ctx.enter_context(nc.Block())
        block.sync(lambda e: sp.emit(e))
        block.gpsimd(lambda e: pool.emit(e))
        block.scalar(lambda e: act.emit(e))
        block.vector(lambda e: dve.emit(e))
        block.tensor(lambda e: pe.emit(e))


def kernel(x, ctx_1024, L0_xattn_Wq, L0_xattn_bq, L0_xattn_Wk, L0_xattn_bk, L0_xattn_Wv, L0_xattn_bv,
           L0_xattn_Wo, L0_xattn_bo, L0_ffn_router_w, L0_ffn_w_fc, L0_ffn_b_fc, L0_ffn_w_proj, L0_ffn_b_proj):
    import concourse.bacc as bacc
    from concourse.bass_utils import run_bass_kernel_spmd

    def columns(w):
        w = np.asarray(w)
        return w.transpose(1, 0, 2).reshape(w.shape[1], -1)

    x = np.asarray(x)
    b_fc = np.asarray(L0_ffn_b_fc)
    arrays = {
        "x": x.reshape(-1, x.shape[-1]),
        "ctx_t": np.asarray(ctx_1024).reshape(-1, x.shape[-1]).T,
        "wq": columns(L0_xattn_Wq), "bq": np.asarray(L0_xattn_bq).reshape(-1, P).T,
        "wk": columns(L0_xattn_Wk), "bk": np.asarray(L0_xattn_bk).reshape(-1, P).T,
        "wv": columns(L0_xattn_Wv), "bv": np.asarray(L0_xattn_bv).reshape(-1),
        "wo": np.asarray(L0_xattn_Wo), "bo": np.asarray(L0_xattn_bo),
        "router_t": np.asarray(L0_ffn_router_w).T,
        "w_fc": np.asarray(L0_ffn_w_fc),
        "b_fc": b_fc.reshape(b_fc.shape[0], -1, P).transpose(2, 0, 1),
        "w_proj": np.asarray(L0_ffn_w_proj), "b_proj": np.asarray(L0_ffn_b_proj),
    }
    arrays = {f"in_{k}": np.ascontiguousarray(v) for k, v in arrays.items()}
    nc = bacc.Bacc("TRN2", target_bir_lowering=False, num_devices=1)
    ins = [nc.dram_tensor(k, v.shape, mybir.dt.from_np(v.dtype), kind="ExternalInput").ap() for k, v in arrays.items()]
    out = nc.dram_tensor("out_y", arrays["in_x"].shape, F32, kind="ExternalOutput").ap()
    xattn_moe_block(nc, *ins, out)
    r = run_bass_kernel_spmd(nc, [arrays], core_ids=[0])
    return r.results[0]["out_y"].reshape(x.shape)
```

```python
from contextlib import ExitStack

import numpy as np

import concourse.bass as bass
from concourse import mybir

F32 = mybir.dt.float32
BF16 = mybir.dt.bfloat16
U32 = mybir.dt.uint32
I32 = mybir.dt.int32
ALU = mybir.AluOpType
ACT = mybir.ActivationFunctionType
AX_X = mybir.AxisListType.X

P = 128
BANK = 512
EPS = 1e-5
PART_PAIRS = [(0, 0), (0, 1), (0, 2), (1, 0), (1, 1), (2, 0)]


class Lane:

    def __init__(self, sem):
        self.sem = sem
        self.count = 0
        self.program = []
        self.passed = {}

    def do(self, fn):
        self.program.append(fn)

    def done(self, fn):
        self.count += 1
        self.program.append(lambda e: fn(e).then_inc(self.sem, 1))
        return (self.sem, self.count)

    def dma(self, fn, sem):
        sem.count += 16
        self.program.append(lambda e: fn(e).then_inc(sem.sem, 16))
        return (sem.sem, sem.count)

    def wait(self, *tokens):
        for sem, value in tokens:
            if self.passed.get(id(sem), 0) < value:
                self.passed[id(sem)] = value
                self.program.append(lambda e, s=sem, v=value: e.wait_ge(s, v))

    def step(self, fn):
        token = self.done(fn)
        self.wait(token)
        return token

    def emit(self, engine):
        for fn in self.program:
            fn(engine)


class DmaCount:
    def __init__(self, sem):
        self.sem = sem
        self.count = 0


def xattn_moe_block(nc, x, ctx_t, wq, bq, wk, bk, wv, bv, wo, bo, router_t, w1, w_proj, b_proj, out):
    N, E = x.shape
    T = ctx_t.shape[1]
    B = 2
    S, TB = N // B, T // B
    H, D = 16, 16
    NE, HID, _ = w_proj.shape
    EC = E // P
    NT = N // P
    TT = T // P
    ST = S // P
    KT = TB // P
    HG = 4
    NG = H // HG
    HPM = P // D
    NPART = 3
    STACK = D * len(PART_PAIRS)
    HC = HID // P
    SCALE = 1.0 / np.sqrt(D)
    TOKEN = E + NE
    ROW = TOKEN + 8
    TOP = 2
    SLOTS = TOP * N // P + NE - 1

    ctx = ExitStack()
    with ctx:
        def sb(name, shape, dt=F32):
            return ctx.enter_context(nc.sbuf_tensor(name, shape, dt))

        def sem(name):
            return ctx.enter_context(nc.semaphore(name))

        x_sb = sb("x_sb", [P, NT, E])
        xn = sb("xn", [P, NT, ROW])
        xT = sb("xT", [P, EC, N])
        ctx_p = sb("ctx_p", [P, EC * T])
        ctxT = ctx_p[:, :].rearrange("p (c t) -> p c t", c=EC)
        prob = ctx_p[:, :].rearrange("p (r h s) -> p r h s", r=2, h=HG)
        wq_sb, wk_sb, wv_sb, wo_sb = (sb(n, [P, EC, E]) for n in ("wq_sb", "wk_sb", "wv_sb", "wo_sb"))
        bq_sb, bk_sb = sb("bq_sb", [P, EC]), sb("bk_sb", [P, EC])
        bv_sb, bo_sb = sb("bv_sb", [P, E]), sb("bo_sb", [P, E])
        k_stack = sb("k_stack", [P, B, H, TB], BF16)
        q_stack = sb("q_stack", [P, H, N], BF16)
        v_ones = sb("v_ones", [P, TT, H, 2 * D])
        parts = sb("parts", [P, 2, NPART, 1024], BF16)
        rest = sb("rest", [P, 2, 1024])
        ident = sb("ident", [P, P])
        ident_b = sb("ident_b", [P, P], BF16)
        eps_sb = sb("eps_sb", [P, 1])
        stats = sb("stats", [P, NT, 6])
        mv = sb("mv", [P, NT, 2])
        rstd = sb("rstd", [P, NT])
        mx_half = sb("mx_half", [P, 2, HG * ST, 2])
        neg_f = sb("neg_f", [P, 2, HG * ST])
        neg_p = sb("neg_p", [P, ST, NPART, HG], BF16)
        negT = rest[0:NPART * HG, 1, S:2 * S].bitcast(BF16).rearrange("p (r s) -> p r s", r=2)
        oT = rest[:, 1, 0:S]
        rsum = sb("rsum", [P, ST * HG])
        keys = k_stack[:, :, :, :].rearrange("p b h t -> p (b h t)").bitcast(F32)
        w_pr_sb = keys[:, 0:NE * HC * E]
        W1 = EC * HID + HC
        vflat = v_ones[:, :, :, :].rearrange("p t h d -> p (t h d)")
        W1_BUFS = vflat.shape[1] // W1
        w1_sb = [vflat[:, r * W1:(r + 1) * W1] for r in range(W1_BUFS)]
        qflat = q_stack[:, :, :].rearrange("p h t -> p (h t)").bitcast(F32)
        X_BUFS = 3
        sizes = [ROW] * X_BUFS + [E] * 2 + [HC * P] * 2 + [E] * 2
        starts = [sum(sizes[:n]) for n in range(len(sizes))]
        assert starts[-1] + sizes[-1] <= qflat.shape[1]
        pieces = [qflat[:, a:a + n] for a, n in zip(starts, sizes)]
        row_sb, pieces = pieces[:X_BUFS], pieces[X_BUFS:]
        rowT = [v.rearrange("p (c t) -> p c t", c=EC) for v in pieces[0:2]]
        hidT = [v.rearrange("p (c t) -> p c t", c=HC) for v in pieces[2:4]]
        y_sb = pieces[4:6]
        b_pr_sb = sb("b_pr_sb", [NE, E])
        spare = parts[:, :, :, :].rearrange("p r a t -> p (r a t)").bitcast(F32)
        used = 0

        def late(shape, dt=F32):
            nonlocal used
            n = int(np.prod(shape[1:]))
            view = spare[:, used:used + n]
            used += n
            view = view if dt == F32 else view.bitcast(dt)
            axes = "abcd"[:len(shape) - 1]
            return view.rearrange(f"p ({' '.join(axes)}) -> p {' '.join(axes)}", **dict(zip(axes, shape[1:])))

        router_sb = sb("router_sb", [P, EC, NE])
        logit = late([P, NT, NE])
        gate = late([P, NT, NE])
        red = late([P, NT])
        top8 = late([P, NT, 8])
        idx8 = late([P, NT, 8], U32)
        idxf = late([P, NT, 2])
        iota_e = sb("iota_e", [P, NE])
        hot = late([P, 2, NT, NE])
        chosen = late([P, NT, NE])
        before = late([P, NT, NE])
        place = late([P, NT, NE])
        picked = late([P, NT, NE])
        slot_f = late([P, TOP, NT])
        slot = late([P, TOP, NT], U32)
        count = late([P, NE])
        multiples = sb("multiples", [P, NE, NT])
        over = late([P, NE, NT])
        tiles = late([P, NE])
        ends = late([P, NE])
        upto = sb("upto", [P, NE, NE])
        upto_t = late([P, NE, NE])
        number = sb("number", [P, SLOTS, NE])
        passed = late([P, SLOTS, NE + 1])
        mine = late([P, SLOTS, NE])
        expert_f = late([P, SLOTS])
        expert = late([P, SLOTS], I32)
        earlier = sb("earlier", [P, P])
        ones = sb("ones", [P, P])
        blank = sb("blank", [P, ROW])
        token_i = sb("token_i", [P, NT + 1], I32)
        wt = sb("wt", [P, 2, NE])
        weight = sb("weight", [P, 2])
        token_u = sb("token_u", [P, X_BUFS], U32)
        combT = rest[0:NE, 0, :]

        ps = ctx.enter_context(nc.psum_tensor("ps", [P, 8, BANK], F32))
        ST_BANKS, MAX_BANKS, O_BANK, MISC = 0, 4, 6, 7

        pe, dve, act, pool, sp = (Lane(sem("s_" + n)) for n in ("pe", "dve", "act", "pool", "sp"))

        def dsem(name):
            return DmaCount(sem(name))

        d_x, d_wk, d_wq, d_wv, d_misc, d_out = (dsem(n) for n in ("d_x", "d_wk", "d_wq", "d_wv", "d_misc", "d_out"))
        d_blank, d_pr, d_sent, d_y0, d_add = (dsem(n) for n in ("d_blank", "d_pr", "d_sent", "d_y0", "d_add"))
        d_w1 = [dsem(f"d_w1_{r}") for r in range(W1_BUFS)]
        d_row = [dsem(f"d_row{r}") for r in range(X_BUFS)]
        d_ctx = [dsem(f"d_ctx{b}") for b in range(B)]
        cv = ctx_t.rearrange("(c p) t -> p c t", p=P)

        def w2(w):
            return w.rearrange("(c p) n -> p c n", p=P)

        got_wk = [sp.dma(lambda e: e.dma_start(wk_sb[:, :, :], w2(wk)), d_wk),
                  sp.dma(lambda e: e.dma_start(bk_sb[:, :], bk), d_wk)][-1]
        got_ctx = [sp.dma(lambda e: e.dma_start(ctxT[:, :, 0:TB], cv[:, :, 0:TB]), d_ctx[0])]
        got_x = act.dma(lambda e: e.dma_start(x_sb[:, :, :], x.rearrange("(i p) e -> p i e", p=P)), d_x)
        got_wq = [act.dma(lambda e: e.dma_start(wq_sb[:, :, :], w2(wq)), d_wq),
                  act.dma(lambda e: e.dma_start(bq_sb[:, :], bq), d_wq)][-1]
        got_ctx.append(sp.dma(lambda e: e.dma_start(ctxT[:, :, TB:T], cv[:, :, TB:T]), d_ctx[1]))
        got_wv = sp.dma(lambda e: e.dma_start(wv_sb[:, :, :], w2(wv)), d_wv)
        for dst, src in ((wo_sb[:, :, :], w2(wo)),
                         (bv_sb[:, :], bv.partition_broadcast(P)), (bo_sb[:, :], bo.partition_broadcast(P)),
                         (router_sb[:, :, :], w2(router_t)), (b_pr_sb[:, :], b_proj)):
            got_misc = sp.dma(lambda e, d=dst, s=src: e.dma_start(d, s), d_misc)

        pool.step(lambda e: e.memset(eps_sb[:, :], EPS))
        for m in (ident, ident_b):
            pool.step(lambda e, m=m: e.memset(m[:, :], 0.0))
            made_ident = pool.step(lambda e, m=m: e.affine_select(
                out=m[:, :], in_=m[:, :], compare_op=ALU.not_equal, fill=1.0, base=0,
                pattern=[[-1, P]], channel_multiplier=1))
        pair_of_ones = float(np.array([0x3F803F80], np.uint32).view(np.float32)[0])
        made_key_ones = pool.step(lambda e: e.memset(
            k_stack[STACK:STACK + NPART, :, :, :].rearrange("p b h t -> p (b h t)").bitcast(F32), pair_of_ones))
        made_v_ones = pool.step(lambda e: e.memset(v_ones[:, :, :, D:2 * D], 1.0))
        for k in range(NE):
            pool.step(lambda e, k=k: e.memset(iota_e[:, k:k + 1], float(k)))
        for k in range(NT):
            pool.step(lambda e, k=k: e.memset(multiples[:, :, k:k + 1], float(P * k)))
        for j in range(SLOTS):
            pool.step(lambda e, j=j: e.memset(number[:, j, :], float(j)))
        for m in (upto, earlier, ones):
            pool.step(lambda e, m=m: e.memset(m[:], 1.0))
        pool.step(lambda e: e.affine_select(out=upto[:, :, :], in_=upto[:, :, :], compare_op=ALU.is_ge, fill=0.0,
                                            base=0, pattern=[[1, NE], [-1, NE]], channel_multiplier=0))
        pool.step(lambda e: e.affine_select(out=earlier[:, :], in_=earlier[:, :], compare_op=ALU.is_ge, fill=0.0,
                                            base=-1, pattern=[[1, P]], channel_multiplier=-1))
        pool.step(lambda e: e.memset(blank[:, :], 0.0))
        pool.step(lambda e: e.iota(token_i[:, :], pattern=[[P, NT + 1]], base=0, channel_multiplier=1))
        made_consts = pool.step(lambda e: e.tensor_copy(blank[:, TOKEN:TOKEN + 1], token_i[:, NT:NT + 1]))

        rows_dram = nc.dram_tensor("rows_dram", [SLOTS * P, ROW], F32, kind="Internal").ap()
        pool.wait(made_consts)
        blanked = pool.dma(lambda e: e.dma_start(
            rows_dram.rearrange("(j p) n -> p j n", p=P),
            blank[:, :].unsqueeze(1).to_broadcast([P, SLOTS, ROW])), d_blank)

        def layernorm(src, ready):
            for i in range(NT):
                dve.wait(*ready[i])
                dve.step(lambda e, i=i: e.bn_stats(stats[:, i, :], src[:, i, :]))
                last = dve.done(lambda e, i=i: e.bn_aggr(mv[:, i, :], stats[:, i, :]))
            act.wait(last, made_ident)
            std = act.done(lambda e: e.activation(rstd[:, :], mv[:, :, 1], ACT.Sqrt, bias=eps_sb[:, :]))
            dve.wait(std)
            dve.step(lambda e: e.reciprocal(rstd[:, :], rstd[:, :]))
            return [dve.done(lambda e, i=i: e.tensor_scalar(
                xn[:, i, 0:E], src[:, i, :], mv[:, i, 0:1], rstd[:, i:i + 1], ALU.subtract, ALU.mult))
                for i in range(NT)]

        normed = layernorm(x_sb, [[got_x]] * NT)

        def transpose_rows(src, dst, ready, banks, free):
            made = []
            for n in range(N // BANK):
                for c in range(EC):
                    bank = banks[(n * EC + c) % len(banks)]
                    pe.wait(*free.get(bank, []), made_ident)
                    for j in range(BANK // P):
                        i = n * (BANK // P) + j
                        pe.wait(ready[i])
                        last = pe.done(lambda e, bank=bank, j=j, i=i, c=c: e.transpose(
                            ps[:, bank, j * P:(j + 1) * P], src[:, i, c * P:(c + 1) * P], ident[:, :]))
                    eng = act if c else dve
                    eng.wait(last)
                    if c:
                        t = act.done(lambda e, bank=bank, n=n, c=c: e.activation(
                            dst[:, c, n * BANK:(n + 1) * BANK], ps[:, bank, :], ACT.Copy))
                    else:
                        t = dve.done(lambda e, bank=bank, n=n, c=c: e.tensor_copy(
                            dst[:, c, n * BANK:(n + 1) * BANK], ps[:, bank, :]))
                    free[bank] = [t]
                    made.append(t)
            return made

        free = {}
        d_parts = [dsem("d_parts0"), dsem("d_parts1")]
        d_stack = [dsem(f"d_stack{n}") for n in range(EC * (B + 1))]
        part_rows = [nc.dram_tensor(f"part_rows{n}", [NPART, P, 1024], BF16, kind="Internal").ap()
                     for n in range(EC * (B + 1))]
        parts_read = [None, None]
        blocks = 0

        def project(w, bias, src, cols, m, ready, stack):
            nonlocal blocks
            r = blocks % 2
            b0 = 2 * r
            blocks += 1
            pe.wait(*ready, *free.get(b0, []), *free.get(b0 + 1, []))
            for n in range(2):
                for c in range(EC):
                    last = pe.done(lambda e, n=n, c=c: e.matmul(
                        ps[:, b0 + n, :], w[:, c, m * P:(m + 1) * P],
                        src[:, c, cols + n * BANK:cols + (n + 1) * BANK], start=c == 0, stop=c == EC - 1))
            block = ps[:, b0:b0 + 2, :].rearrange("p a b -> p (a b)")
            act.wait(last)
            if parts_read[r]:
                act.wait(parts_read[r])
            p1 = act.done(lambda e: e.activation(parts[:, r, 0, :], block, ACT.Identity, bias=bias[:, m:m + 1]))
            dve.wait(p1)
            left = dve.step(lambda e: e.scalar_tensor_tensor(
                rest[:, r, :], block, bias[:, m:m + 1], parts[:, r, 0, :], ALU.add, ALU.subtract))
            free[b0] = free[b0 + 1] = [left]
            act.wait(left)
            p2 = act.done(lambda e: e.activation(parts[:, r, 1, :], rest[:, r, :], ACT.Copy))
            dve.wait(p2)
            p3 = dve.done(lambda e: e.tensor_tensor(
                parts[:, r, 2, :], rest[:, r, :], parts[:, r, 1, :], ALU.subtract))
            sp.wait(p1, p2, p3)
            slot = blocks - 1
            kept = sp.dma(lambda e: e.dma_start(
                part_rows[slot].rearrange("a (d h) t -> (d h) a t", d=D), parts[:, r, :, :]), d_parts[r])
            parts_read[r] = kept
            sp.wait(kept)
            return stack(part_rows[slot].rearrange("a (d h) t -> (a d) h t", d=D), m)

        k_ready, q_ready = {}, {}

        def fill(dst, src, rows, first, m):
            n = src.shape[0] if rows is None else rows.stop - rows.start
            return sp.dma(lambda e: e.dma_start(
                dst[first:first + n, m * HPM:(m + 1) * HPM, :], src if rows is None else src[rows]), d_stack[blocks - 1])

        def stack_keys(b):
            return lambda src, m: [fill(k_stack[:, b, :, :], src, slice(0, D * n), D * first, m)
                                   for first, n in ((0, 3), (3, 2), (5, 1))][-1]

        def stack_queries(src, m):
            return [fill(q_stack, src, slice(D * part, D * (part + 1)), D * g, m)
                    for g, (part, _) in enumerate(PART_PAIRS)][-1]

        def k_block(b, m):
            k_ready[b, m] = project(wk_sb, bk_sb, ctxT, b * TB, m, [got_wk, got_ctx[b]], stack_keys(b))

        def q_block(m):
            q_ready[m] = project(wq_sb, bq_sb, xT, 0, m, [got_wq] + xT_made, stack_queries)

        act.wait(got_wk)
        k_block(0, 0)
        xT_made = transpose_rows(xn, xT, normed, [4, 5, 6, 7], free)
        act.wait(got_wq)
        q_block(0)
        k_block(0, 1)
        q_block(1)
        k_block(1, 0)
        k_block(1, 1)

        pe.wait(got_wv)
        for t in range(TT):
            bank = 6 + t % 2
            pe.wait(*free.get(bank, []))
            for c in range(EC):
                last = pe.done(lambda e, t=t, c=c, bank=bank: e.matmul(
                    ps[:, bank, 0:E], ctxT[:, c, t * P:(t + 1) * P], wv_sb[:, c, :], start=c == 0, stop=c == EC - 1))
            act.wait(last)
            v_made = act.done(lambda e, t=t, bank=bank: e.activation(
                v_ones[:, t, :, 0:D], ps[:, bank, 0:E].rearrange("p (h d) -> p h d", h=H), ACT.Copy))
            free[bank] = [v_made]

        groups = B * NG
        units = [(g, hh, i, n) for g in range(groups) for hh in range(HG) for i in range(ST) for n in range(TB // BANK)]
        per_group = len(units) // groups
        per_step = per_group // KT
        LEAD = per_group + per_group // 2
        emitted = 0
        max_read = [free.get(MAX_BANKS, []), free.get(MAX_BANKS + 1, [])]
        neg_made, negT_ready = {}, {}
        d_neg = [dsem("d_neg0"), dsem("d_neg1")]
        misc_read = free.get(MISC, [])

        def heads(g):
            return [HG * (g % NG) + hh for hh in range(HG)]

        def max_unit():
            nonlocal emitted
            g, hh, i, n = units[emitted]
            b, h = g // NG, heads(g)[hh]
            s = emitted % 2
            bank = MAX_BANKS + s
            pe.wait(k_ready[b, h // HPM], q_ready[h // HPM], *max_read[s])
            q0 = b * S + i * P
            made = pe.done(lambda e: e.matmul(ps[:, bank, :], q_stack[0:STACK, h, q0:q0 + P],
                                              k_stack[0:STACK, b, h, n * BANK:(n + 1) * BANK], start=True, stop=True))
            dve.wait(made)
            t = dve.done(lambda e: e.tensor_reduce(mx_half[:, g % 2, hh * ST + i, n:n + 1], ps[:, bank, :],
                                                   AX_X, ALU.max))
            max_read[s] = [t]
            emitted += 1
            if emitted % per_group == 0:
                negate(g, t)

        def negate(g, last_max):
            r = g % 2
            nf = neg_f[:, r, :]
            dve.wait(last_max)
            dve.step(lambda e: e.tensor_reduce(nf, mx_half[:, r, :, :], AX_X, ALU.max, negate=True))
            if g >= 1:
                dve.wait(neg_transposed[g - 1])
            for part in range(NPART):
                view = neg_p[:, :, part, :].rearrange("p i h -> p h i")
                src = nf.rearrange("p (h i) -> p h i", h=HG)
                t = dve.step(lambda e, v=view, s=src: e.tensor_copy(v, s))
                if part < NPART - 1:
                    dve.step(lambda e, v=view, s=src: e.tensor_tensor(s, s, v, ALU.subtract))
            neg_made[g] = t

        neg_transposed = {}

        def spread_max(g):
            nonlocal misc_read
            r = g % 2
            bankT = ps[0:NPART * HG, MISC, 0:S // 2].bitcast(BF16)
            pe.wait(neg_made[g], made_ident, *misc_read)
            for i in range(ST):
                t = pe.done(lambda e, i=i: e.transpose(
                    bankT[:, i * P:(i + 1) * P], neg_p[:, i, :, :].rearrange("p a h -> p (a h)"), ident_b[:, :]))
            neg_transposed[g] = t
            act.wait(t)
            if g >= 2:
                act.wait(negT_ready[g - 2])
            moved = act.done(lambda e: e.activation(negT[:, r, :], bankT, ACT.Copy))
            misc_read = [moved]
            sp.wait(moved)
            b = g // NG
            for hh, h in enumerate(heads(g)):
                negT_ready[g] = sp.dma(lambda e, hh=hh, h=h: e.dma_start(
                    q_stack[STACK:STACK + NPART, h, b * S:(b + 1) * S], negT[hh:NPART * HG:HG, r, :]), d_neg[r])

        exp_done = {}
        pv_done = {}
        st_read = [free.get(0, []) + free.get(1, []), free.get(2, []) + free.get(3, [])]

        def score_pair(g, j, u):
            b = g // NG
            step = g * KT + j
            pe.wait(made_key_ones, negT_ready[g], *st_read[u])
            for a in range(2):
                h = heads(g)[2 * u + a]
                made = pe.done(lambda e, a=a, h=h: e.matmul(
                    ps[:, ST_BANKS + 2 * u + a, :], k_stack[0:STACK + NPART, b, h, j * P:(j + 1) * P],
                    q_stack[0:STACK + NPART, h, b * S:(b + 1) * S], start=True, stop=True))
            act.wait(made)
            if step >= 2:
                act.wait(pv_done[step - 2])
            t = act.done(lambda e: e.activation(
                prob[:, step % 2, 2 * u:2 * u + 2, :], ps[:, ST_BANKS + 2 * u:ST_BANKS + 2 * u + 2, :],
                ACT.Exp, scale=float(SCALE)))
            st_read[u] = [t]
            exp_done[step, u] = t

        o_read = free.get(O_BANK, [])

        def weighted_values(step):
            nonlocal o_read
            g, j = step // KT, step % KT
            b = g // NG
            pe.wait(v_made, made_v_ones, exp_done[step, 0], exp_done[step, 1])
            if j == 0:
                pe.wait(*o_read)
            for hh, h in enumerate(heads(g)):
                t = pe.done(lambda e, hh=hh, h=h: e.matmul(
                    ps[2 * D * hh:2 * D * (hh + 1), O_BANK, :], v_ones[:, b * KT + j, h, :],
                    prob[:, step % 2, hh, :], start=j == 0, stop=j == KT - 1))
            pv_done[step] = t
            if j == KT - 1:
                act.wait(t)
                if g >= 1:
                    act.wait(oT_read[g - 1])
                o_moved[g] = act.done(lambda e: e.activation(oT, ps[:, O_BANK, :], ACT.Copy))
                o_read = [o_moved[g]]

        oT_read, o_moved, attn_made = {}, {}, {}

        def normalise(g):
            nonlocal misc_read
            b = g // NG
            pe.wait(o_moved[g], *misc_read)
            for i in range(ST):
                t = pe.done(lambda e, i=i: e.transpose(
                    ps[:, MISC, i * P:(i + 1) * P], oT[:, i * P:(i + 1) * P], ident[:, :]))
            oT_read[g] = t
            rows = ps[:, MISC, :].rearrange("p (i h d) -> p i h d", i=ST, h=HG)
            h0 = HG * (g % NG) * D
            dst = xn[:, b * ST:(b + 1) * ST, h0:h0 + HG * D].rearrange("p i (h d) -> p i h d", h=HG)
            rs = rsum[:, :].rearrange("p (i h) -> p i h", i=ST)
            dve.wait(t)
            dve.step(lambda e: e.reciprocal(rs, rows[:, :, :, D]))
            for i in range(ST):
                a = dve.done(lambda e, i=i: e.tensor_tensor(
                    dst[:, i, :, :], rows[:, i, :, 0:D],
                    rs[:, i, :].unsqueeze(2).to_broadcast([P, HG, D]), ALU.mult))
            attn_made[g] = a
            misc_read = [a]

        for _ in range(LEAD):
            max_unit()
            if emitted == per_group + 4:
                spread_max(0)
        for step in range(groups * KT):
            g, j = step // KT, step % KT
            score_pair(g, j, 0)
            for k in range(per_step):
                if k == per_step // 2:
                    score_pair(g, j, 1)
                if emitted < len(units):
                    max_unit()
            if step >= 1:
                weighted_values(step - 1)
            if j == 2 and g >= 1:
                normalise(g - 1)
            if j == 5 and g + 1 < groups:
                spread_max(g + 1)
        weighted_values(groups * KT - 1)
        normalise(groups - 1)

        pr = w_proj.rearrange("x (c p) n -> x p c n", p=P)
        for b in range(B):
            sp.wait(pv_done[(b + 1) * NG * KT - 1])
            for x_ in range(b * NE // B, (b + 1) * NE // B):
                w_pr_got = sp.dma(lambda e, x_=x_: e.dma_start(
                    w_pr_sb[:, x_ * HC * E:(x_ + 1) * HC * E].rearrange("p (c n) -> p c n", c=HC), pr[x_]), d_pr)

        pool.wait(got_misc, got_x, normed[-1])
        x_bo = None
        for i in range(NT):
            x_bo = pool.step(lambda e, i=i: e.tensor_tensor(x_sb[:, i, :], x_sb[:, i, :], bo_sb[:, :], ALU.add))
        dve.wait(attn_made[groups - 1], got_misc)
        attn_bv = [dve.done(lambda e, i=i: e.tensor_tensor(xn[:, i, 0:E], xn[:, i, 0:E], bv_sb[:, :], ALU.add))
                   for i in range(NT)]
        free = {ST_BANKS: st_read[0], ST_BANKS + 1: st_read[0], ST_BANKS + 2: st_read[1], ST_BANKS + 3: st_read[1],
                MAX_BANKS: max_read[0], MAX_BANKS + 1: max_read[1], O_BANK: o_read, MISC: misc_read}
        attnT_made = transpose_rows(xn, xT, attn_bv, [0, 1, 2, 3], free)
        x1_made = []
        for i in range(NT):
            bank = 4 + i % 4
            pe.wait(*free[bank], *attnT_made)
            for c in range(EC):
                last = pe.done(lambda e, i=i, c=c, bank=bank: e.matmul(
                    ps[:, bank, 0:E], xT[:, c, i * P:(i + 1) * P], wo_sb[:, c, :], start=c == 0, stop=c == EC - 1))
            dve.wait(last, x_bo)
            t = dve.done(lambda e, i=i, bank=bank: e.tensor_tensor(
                x_sb[:, i, :], ps[:, bank, 0:E], x_sb[:, i, :], ALU.add))
            free[bank] = [t]
            x1_made.append(t)

        h2_made = layernorm(x_sb, [[t] for t in x1_made])
        h2T_made = transpose_rows(xn, xT, h2_made, [0, 1, 2, 3], free)
        pe.wait(*h2T_made, *free[4], got_misc)
        for i in range(NT):
            for c in range(EC):
                last = pe.done(lambda e, i=i, c=c: e.matmul(
                    ps[:, 4, i * NE:(i + 1) * NE], xT[:, c, i * P:(i + 1) * P], router_sb[:, c, :],
                    start=c == 0, stop=c == EC - 1))
        lg = ps[:, 4, 0:NT * NE].rearrange("p (i e) -> p i e", i=NT)

        def over_experts(t):
            return t.unsqueeze(2).to_broadcast([P, NT, NE])

        dve.wait(last, made_consts)
        dve.step(lambda e: e.tensor_reduce(red[:, :], lg, AX_X, ALU.max))
        t = dve.step(lambda e: e.tensor_tensor(logit[:, :, :], lg, over_experts(red[:, :]), ALU.subtract))
        free[4] = [t]
        act.wait(t)
        t = act.done(lambda e: e.activation(gate[:, :, :], logit[:, :, :], ACT.Exp))
        dve.wait(t)
        dve.step(lambda e: e.tensor_reduce(red[:, :], gate[:, :, :], AX_X, ALU.add))
        dve.step(lambda e: e.reciprocal(red[:, :], red[:, :]))
        dve.step(lambda e: e.tensor_tensor(gate[:, :, :], gate[:, :, :], over_experts(red[:, :]), ALU.mult))
        for i in range(NT):
            dve.step(lambda e, i=i: e.max(top8[:, i, :], gate[:, i, :]))
            dve.step(lambda e, i=i: e.max_index(idx8[:, i, :], top8[:, i, :], gate[:, i, :]))
        dve.step(lambda e: e.tensor_copy(idxf[:, :, :], idx8[:, :, 0:2]))
        dve.step(lambda e: e.tensor_tensor(red[:, :], top8[:, :, 0], top8[:, :, 1], ALU.add))
        dve.step(lambda e: e.reciprocal(red[:, :], red[:, :]))
        dve.step(lambda e: e.tensor_tensor(top8[:, :, 0:2], top8[:, :, 0:2],
                                           red[:, :].unsqueeze(2).to_broadcast([P, NT, 2]), ALU.mult))
        for a in range(2):
            dve.step(lambda e, a=a: e.tensor_tensor(hot[:, a, :, :], iota_e[:, :].unsqueeze(1).to_broadcast([P, NT, NE]),
                                                    over_experts(idxf[:, :, a]), ALU.is_equal))
        chose = dve.step(lambda e: e.tensor_tensor(chosen[:, :, :], hot[:, 0, :, :], hot[:, 1, :, :], ALU.add))

        pe.wait(chose, made_consts, *free[7])
        flat = chosen[:, :, :].rearrange("p i e -> p (i e)")
        pe.done(lambda e: e.matmul(ps[:, 7, 0:NT * NE], earlier[:, :], flat, start=True, stop=True))
        ranked = pe.done(lambda e: e.matmul(ps[:, 7, NT * NE:2 * NT * NE], ones[:, :], flat, start=True, stop=True))
        rank = ps[:, 7, 0:NT * NE].rearrange("p (i e) -> p i e", i=NT)
        total = ps[:, 7, NT * NE:2 * NT * NE].rearrange("p (i e) -> p i e", i=NT)
        dve.wait(ranked)
        dve.step(lambda e: e.memset(before[:, 0, :], 0.0))
        dve.step(lambda e: e.memset(passed[:, :, 0:1], 1.0))
        for i in range(1, NT):
            dve.step(lambda e, i=i: e.tensor_tensor(before[:, i, :], before[:, i - 1, :], total[:, i - 1, :], ALU.add))
        dve.step(lambda e: e.tensor_tensor(count[:, :], before[:, NT - 1, :], total[:, NT - 1, :], ALU.add))
        dve.step(lambda e: e.tensor_tensor(over[:, :, :], count[:, :].unsqueeze(2).to_broadcast([P, NE, NT]),
                                           multiples[:, :, :], ALU.is_gt))
        dve.step(lambda e: e.tensor_reduce(tiles[:, :], over[:, :, :], AX_X, ALU.add))
        dve.step(lambda e: e.tensor_tensor(upto_t[:, :, :], upto[:, :, :],
                                           tiles[:, :].unsqueeze(1).to_broadcast([P, NE, NE]), ALU.mult))
        dve.step(lambda e: e.tensor_reduce(ends[:, :], upto_t[:, :, :], AX_X, ALU.add))
        dve.step(lambda e: e.tensor_tensor(passed[:, :, 1:NE + 1], number[:, :, :],
                                           ends[:, :].unsqueeze(1).to_broadcast([P, SLOTS, NE]), ALU.is_ge))
        dve.step(lambda e: e.tensor_reduce(expert_f[:, :], passed[:, :, 1:NE + 1], AX_X, ALU.add))
        expert_known = dve.step(lambda e: e.tensor_scalar(
            expert[:, :], expert_f[:, :], float(NE - 1), None, ALU.min))
        dve.step(lambda e: e.tensor_tensor(count[:, :], ends[:, :], tiles[:, :], ALU.subtract))
        dve.step(lambda e: e.tensor_scalar(count[:, :], count[:, :], float(P), None, ALU.mult))
        dve.step(lambda e: e.tensor_tensor(place[:, :, :], before[:, :, :], rank, ALU.add))
        dve.step(lambda e: e.tensor_tensor(place[:, :, :], place[:, :, :],
                                           count[:, :].unsqueeze(1).to_broadcast([P, NT, NE]), ALU.add))
        for a in range(TOP):
            dve.step(lambda e, a=a: e.tensor_tensor(picked[:, :, :], place[:, :, :], hot[:, a, :, :], ALU.mult))
            t = dve.step(lambda e, a=a: e.tensor_reduce(slot_f[:, a, :], picked[:, :, :], AX_X, ALU.add))
        slots_known = dve.step(lambda e: e.tensor_copy(slot[:, :, :], slot_f[:, :, :]))
        free[7] = [slots_known]
        for a in range(TOP):
            dve.step(lambda e, a=a: e.tensor_tensor(hot[:, a, :, :], hot[:, a, :, :],
                                                    over_experts(top8[:, :, a]), ALU.mult))
        dve.step(lambda e: e.tensor_tensor(xn[:, :, E:TOKEN], hot[:, 0, :, :], hot[:, 1, :, :], ALU.add))
        dve.step(lambda e: e.memset(xn[:, :, TOKEN + 1:ROW], 0.0))
        comb_made = dve.step(lambda e: e.tensor_copy(xn[:, :, TOKEN:TOKEN + 1], token_i[:, 0:NT].unsqueeze(2)))
        dve.done(lambda e: e.tensor_tensor(mine[:, :, :], passed[:, :, 0:NE], passed[:, :, 1:NE + 1], ALU.subtract))

        pool.wait(comb_made, slots_known, blanked)
        for i in range(NT):
            for a in range(TOP):
                sent = pool.dma(lambda e, i=i, a=a: e.indirect_dma_start(
                    out=rows_dram, out_offset=bass.IndirectOffsetOnAxis(ap=slot[:, a, i:i + 1], axis=0),
                    in_=xn[:, i, :], in_offset=None), d_sent)

        for n in range(2):
            bank = 5 + n
            pe.wait(comb_made, *free[bank])
            for j in range(4):
                last = pe.done(lambda e, j=j, n=n, bank=bank: e.transpose(
                    ps[0:NE, bank, j * P:(j + 1) * P], xn[:, 4 * n + j, E:TOKEN], ident[:, :]))
            act.wait(last)
            t = act.done(lambda e, n=n, bank=bank: e.activation(
                combT[:, n * BANK:(n + 1) * BANK], ps[0:NE, bank, :], ACT.Copy))
            free[bank] = [t]
            pe.wait(t)
        y_made = [None] * NT
        for i in range(NT):
            bank = 4 + i % 4
            pe.wait(*free[bank])
            last = pe.done(lambda e, i=i, bank=bank: e.matmul(
                ps[:, bank, 0:E], combT[:, i * P:(i + 1) * P], b_pr_sb[:, :], start=True, stop=True))
            dve.wait(last)
            y_made[i] = dve.done(lambda e, i=i, bank=bank: e.tensor_tensor(
                x_sb[:, i, :], ps[:, bank, 0:E], x_sb[:, i, :], ALU.add))
            free[bank] = [y_made[i]]

        y_rows = out.rearrange("(i p) e -> i p e", p=P)
        sp.wait(*y_made)
        for i in range(NT):
            y_kept = sp.dma(lambda e, i=i: e.dma_start(y_rows[i], x_sb[:, i, :]), d_y0)
        y_kept = sp.dma(lambda e: e.dma_start(y_rows[NT], blank[:, 0:E]), d_y0)

        w1_used, rows_used, row_turned, hid_used, y_sent = {}, {}, {}, {}, {}
        w1_got, row_got = {}, {}
        q_free = pv_done[groups * KT - 1]
        attention_free = [q_free, exp_done[groups * KT - 1, 1]]

        def fetch(j):
            r, x_ = j % W1_BUFS, j % X_BUFS
            if j == 0:
                sp.wait(expert_known, *attention_free)
            if j >= W1_BUFS:
                sp.wait(w1_used[j - W1_BUFS])
            def first_layer(e):
                which = e.value_load(expert[0:1, j:j + 1], min_val=0, max_val=NE - 1)
                return e.dma_start(w1_sb[r], w1[bass.ds(which, 1), :, :].rearrange("a p n -> p (a n)"))
            w1_got[j] = sp.dma(first_layer, d_w1[r])
            sp.wait(sent)
            if j >= X_BUFS:
                sp.wait(*rows_used[j - X_BUFS])
            row_got[j] = sp.dma(lambda e: e.dma_start(row_sb[x_], rows_dram[j * P:(j + 1) * P, :]), d_row[x_])

        def hidden(j):
            r, x_, a = j % W1_BUFS, j % X_BUFS, j % 2
            tb = 6 + a
            pe.wait(row_got[j], *free[tb])
            for c in range(EC):
                t = pe.done(lambda e, c=c: e.transpose(
                    ps[:, tb, c * P:(c + 1) * P], row_sb[x_][:, c * P:(c + 1) * P], ident[:, :]))
            dve.wait(t)
            if j >= 2:
                dve.wait(w1_used[j - 2])
            turned = dve.done(lambda e: e.tensor_copy(
                rowT[a], ps[:, tb, 0:E].rearrange("p (c t) -> p c t", c=EC)))
            free[tb] = [turned]
            dve.wait(row_got[j])
            dve.step(lambda e: e.tensor_tensor(wt[:, a, :], row_sb[x_][:, E:TOKEN], mine[:, j, :], ALU.mult))
            weighed = dve.step(lambda e: e.tensor_reduce(weight[:, a:a + 1], wt[:, a, :], AX_X, ALU.add))
            if j >= X_BUFS:
                dve.wait(y_sent[j - X_BUFS])
            numbered = dve.done(lambda e: e.tensor_copy(token_u[:, x_:x_ + 1], row_sb[x_][:, TOKEN:TOKEN + 1]))
            rows_used[j] = [t, numbered]
            pe.wait(turned, w1_got[j])
            w1v = w1_sb[r][:, 0:EC * HID].rearrange("p (c h) -> p c h", c=EC)
            if j >= 2:
                act.wait(hid_used[j - 2])
            for n in range(2):
                bank = 2 * a + n
                pe.wait(*free[bank])
                for q in range(HC // 2):
                    c2 = n * (HC // 2) + q
                    for c in range(EC):
                        last = pe.done(lambda e, q=q, c2=c2, c=c, bank=bank: e.matmul(
                            ps[:, bank, q * P:(q + 1) * P], w1v[:, c, c2 * P:(c2 + 1) * P], rowT[a][:, c, :],
                            start=c == 0, stop=c == EC - 1))
                act.wait(last)
                for q in range(HC // 2):
                    c2 = n * (HC // 2) + q
                    t = act.done(lambda e, q=q, c2=c2, bank=bank: e.activation(
                        hidT[a][:, c2, :], ps[:, bank, q * P:(q + 1) * P], ACT.Gelu_apprx_tanh,
                        bias=w1_sb[r][:, EC * HID + c2:EC * HID + c2 + 1]))
                free[bank] = [t]
            w1_used[j] = t
            return t

        def second_layer(j, made):
            a = j % 2
            bank = 4 + a
            pe.wait(made, w_pr_got, *free[bank])
            here = {}
            pe.do(lambda e: here.update(which=e.value_load(expert[0:1, j:j + 1], min_val=0, max_val=NE - 1)))
            for c2 in range(HC):
                last = pe.done(lambda e, c2=c2: e.matmul(
                    ps[:, bank, 0:E], hidT[a][:, c2, :],
                    w_pr_sb[:, bass.ds(here["which"] * (HC * E) + c2 * E, E)], start=c2 == 0, stop=c2 == HC - 1))
            hid_used[j] = last
            dve.wait(last)
            if j >= 2:
                dve.wait(y_sent[j - 2])
            scaled = dve.done(lambda e: e.tensor_scalar(
                y_sb[a], ps[:, bank, 0:E], weight[:, a:a + 1], None, ALU.mult))
            free[bank] = [scaled]
            pool.wait(scaled, y_kept)
            if j >= 1:
                pool.wait(y_sent[j - 1])
            y_sent[j] = pool.dma(lambda e: e.indirect_dma_start(
                out=out, out_offset=bass.IndirectOffsetOnAxis(ap=token_u[:, j % X_BUFS:j % X_BUFS + 1], axis=0),
                in_=y_sb[a], in_offset=None, compute_op=ALU.add), d_add)

        hid_made = {}
        pe.wait(expert_known)
        for j in range(SLOTS):
            fetch(j)
            hid_made[j] = hidden(j)
            if j >= 1:
                second_layer(j - 1, hid_made[j - 1])
        second_layer(SLOTS - 1, hid_made[SLOTS - 1])
        pool.wait(y_sent[SLOTS - 1])
        sp.wait(y_kept, y_sent[SLOTS - 1])

        block = ctx.enter_context(nc.Block())
        block.sync(lambda e: sp.emit(e))
        block.gpsimd(lambda e: pool.emit(e))
        block.scalar(lambda e: act.emit(e))
        block.vector(lambda e: dve.emit(e))
        block.tensor(lambda e: pe.emit(e))


def kernel(x, ctx_1024, L0_xattn_Wq, L0_xattn_bq, L0_xattn_Wk, L0_xattn_bk, L0_xattn_Wv, L0_xattn_bv,
           L0_xattn_Wo, L0_xattn_bo, L0_ffn_router_w, L0_ffn_w_fc, L0_ffn_b_fc, L0_ffn_w_proj, L0_ffn_b_proj):
    import concourse.bacc as bacc
    from concourse.bass_utils import run_bass_kernel_spmd

    def columns(w):
        w = np.asarray(w)
        return w.transpose(1, 0, 2).reshape(w.shape[1], -1)

    x = np.asarray(x)
    w_fc, b_fc = np.asarray(L0_ffn_w_fc), np.asarray(L0_ffn_b_fc)
    n_exp, n_feat, n_hid = w_fc.shape
    w1 = np.concatenate([
        w_fc.reshape(n_exp, n_feat // P, P, n_hid).transpose(0, 2, 1, 3).reshape(n_exp, P, -1),
        b_fc.reshape(n_exp, -1, P).transpose(0, 2, 1)], axis=2)
    def by_dim(w):
        w = np.asarray(w)
        return w.reshape(2, 8, -1, w.shape[-1]).transpose(2, 0, 3, 1)

    arrays = {
        "x": x.reshape(-1, x.shape[-1]),
        "ctx_t": np.asarray(ctx_1024).reshape(-1, x.shape[-1]).T,
        "wq": by_dim(L0_xattn_Wq).reshape(x.shape[-1], -1), "bq": by_dim(L0_xattn_bq).reshape(2, P).T,
        "wk": by_dim(L0_xattn_Wk).reshape(x.shape[-1], -1), "bk": by_dim(L0_xattn_bk).reshape(2, P).T,
        "wv": columns(L0_xattn_Wv), "bv": np.asarray(L0_xattn_bv).reshape(-1),
        "wo": np.asarray(L0_xattn_Wo), "bo": np.asarray(L0_xattn_bo),
        "router_t": np.asarray(L0_ffn_router_w).T,
        "w1": w1,
        "w_proj": np.asarray(L0_ffn_w_proj), "b_proj": np.asarray(L0_ffn_b_proj),
    }
    arrays = {f"in_{k}": np.ascontiguousarray(v) for k, v in arrays.items()}
    nc = bacc.Bacc("TRN2", target_bir_lowering=False, num_devices=1)
    ins = [nc.dram_tensor(k, v.shape, mybir.dt.from_np(v.dtype), kind="ExternalInput").ap() for k, v in arrays.items()]
    tokens, features = arrays["in_x"].shape
    out = nc.dram_tensor("out_y", (tokens + P, features), F32, kind="ExternalOutput").ap()
    xattn_moe_block(nc, *ins, out)
    r = run_bass_kernel_spmd(nc, [arrays], core_ids=[0])
    return r.results[0]["out_y"][:tokens].reshape(x.shape)
```

```python
from contextlib import ExitStack

import numpy as np

import concourse.bass as bass
from concourse import mybir

F32 = mybir.dt.float32
BF16 = mybir.dt.bfloat16
U32 = mybir.dt.uint32
I32 = mybir.dt.int32
ALU = mybir.AluOpType
ACT = mybir.ActivationFunctionType
AX_X = mybir.AxisListType.X

P = 128
BANK = 512
EPS = 1e-5
PART_PAIRS = [(0, 0), (0, 1), (0, 2), (1, 0), (1, 1), (2, 0)]


class Lane:

    def __init__(self, sem):
        self.sem = sem
        self.count = 0
        self.program = []
        self.passed = {}

    def do(self, fn):
        self.program.append(fn)

    def done(self, fn):
        self.count += 1
        self.program.append(lambda e: fn(e).then_inc(self.sem, 1))
        return (self.sem, self.count)

    def dma(self, fn, sem):
        sem.count += 16
        self.program.append(lambda e: fn(e).then_inc(sem.sem, 16))
        return (sem.sem, sem.count)

    def wait(self, *tokens):
        for sem, value in tokens:
            if self.passed.get(id(sem), 0) < value:
                self.passed[id(sem)] = value
                self.program.append(lambda e, s=sem, v=value: e.wait_ge(s, v))

    def step(self, fn):
        token = self.done(fn)
        self.wait(token)
        return token

    def emit(self, engine):
        for fn in self.program:
            fn(engine)


class DmaCount:
    def __init__(self, sem):
        self.sem = sem
        self.count = 0


def xattn_moe_block(nc, x, ctx_t, wq, bq, wk, bk, wv, bv, wo, bo, router_t, w1, w_proj, b_proj, out):
    N, E = x.shape
    T = ctx_t.shape[1]
    B = 2
    S, TB = N // B, T // B
    H, D = 16, 16
    NE, HID, _ = w_proj.shape
    EC = E // P
    NT = N // P
    TT = T // P
    ST = S // P
    KT = TB // P
    HG = 4
    NG = H // HG
    HPM = P // D
    NPART = 3
    STACK = D * len(PART_PAIRS)
    HC = HID // P
    SCALE = 1.0 / np.sqrt(D)
    TOKEN = E + NE
    ROW = TOKEN + 8
    TOP = 2
    SLOTS = TOP * N // P + NE - 1

    ctx = ExitStack()
    with ctx:
        def sb(name, shape, dt=F32):
            return ctx.enter_context(nc.sbuf_tensor(name, shape, dt))

        def sem(name):
            return ctx.enter_context(nc.semaphore(name))

        x_sb = sb("x_sb", [P, NT, E])
        xn = sb("xn", [P, NT, ROW])
        xT = sb("xT", [P, EC, N])
        ctx_p = sb("ctx_p", [P, EC * T])
        ctxT = ctx_p[:, :].rearrange("p (c t) -> p c t", c=EC)
        prob = ctx_p[:, :].rearrange("p (r h s) -> p r h s", r=2, h=HG)
        wq_sb, wk_sb, wv_sb, wo_sb = (sb(n, [P, EC, E]) for n in ("wq_sb", "wk_sb", "wv_sb", "wo_sb"))
        bq_sb, bk_sb = sb("bq_sb", [P, EC]), sb("bk_sb", [P, EC])
        bv_sb, bo_sb = sb("bv_sb", [P, E]), sb("bo_sb", [P, E])
        k_stack = sb("k_stack", [P, B, H, TB], BF16)
        q_stack = sb("q_stack", [P, H, N], BF16)
        v_ones = sb("v_ones", [P, TT, H, 2 * D])
        parts = sb("parts", [P, 2, NPART, 1024], BF16)
        rest = sb("rest", [P, 2, 1024])
        ident = sb("ident", [P, P])
        ident_b = sb("ident_b", [P, P], BF16)
        eps_sb = sb("eps_sb", [P, 1])
        unused = sb("unused", [P, 1])
        stats = sb("stats", [P, NT, 6])
        mv = sb("mv", [P, NT, 2])
        rstd = sb("rstd", [P, NT])
        mx_half = sb("mx_half", [P, 2, HG * ST, 2])
        neg_f = sb("neg_f", [P, 2, HG * ST])
        neg_p = sb("neg_p", [P, ST, NPART, HG], BF16)
        negT = sb("negT", [NPART * HG, 2, S], BF16)
        oT = rest[:, 1, 0:S]
        rsum = sb("rsum", [P, ST * HG])
        keys = k_stack[:, :, :, :].rearrange("p b h t -> p (b h t)").bitcast(F32)
        w_pr_sb = keys[:, 0:NE * HC * E]
        W1 = EC * HID + HC
        vflat = v_ones[:, :, :, :].rearrange("p t h d -> p (t h d)")
        W1_BUFS = vflat.shape[1] // W1
        w1_sb = [vflat[:, r * W1:(r + 1) * W1] for r in range(W1_BUFS)]
        qflat = q_stack[:, :, :].rearrange("p h t -> p (h t)").bitcast(F32)
        X_BUFS = 3
        sizes = [ROW] * X_BUFS + [E] * 2 + [HC * P] * 2 + [E] * 2
        starts = [sum(sizes[:n]) for n in range(len(sizes))]
        assert starts[-1] + sizes[-1] <= qflat.shape[1]
        pieces = [qflat[:, a:a + n] for a, n in zip(starts, sizes)]
        row_sb, pieces = pieces[:X_BUFS], pieces[X_BUFS:]
        rowT = [v.rearrange("p (c t) -> p c t", c=EC) for v in pieces[0:2]]
        hidT = [v.rearrange("p (c t) -> p c t", c=HC) for v in pieces[2:4]]
        y_sb = pieces[4:6]
        b_pr_sb = sb("b_pr_sb", [NE, E])
        spare = parts[:, :, :, :].rearrange("p r a t -> p (r a t)").bitcast(F32)
        used = 0

        def late(shape, dt=F32):
            nonlocal used
            n = int(np.prod(shape[1:]))
            view = spare[:, used:used + n]
            used += n
            view = view if dt == F32 else view.bitcast(dt)
            axes = "abcd"[:len(shape) - 1]
            return view.rearrange(f"p ({' '.join(axes)}) -> p {' '.join(axes)}", **dict(zip(axes, shape[1:])))

        router_sb = sb("router_sb", [P, EC, NE])
        logit = late([P, NT, NE])
        gate = late([P, NT, NE])
        red = late([P, NT])
        top8 = late([P, NT, 8])
        idx8 = late([P, NT, 8], U32)
        idxf = late([P, NT, 2])
        iota_e = late([P, NE])
        hot = late([P, 2, NT, NE])
        chosen = late([P, NT, NE // 2]).rearrange("p i e -> p (i e)").bitcast(BF16).rearrange(
            "p (i e) -> p i e", i=NT)
        before = late([P, B + 1, NE])
        place = late([P, NT, NE])
        picked = late([P, NT, NE])
        slot_f = late([P, TOP, NT])
        slot = late([P, TOP, NT], U32)
        count = late([P, NE])
        first = late([P, NE])
        sel = late([P, SLOTS, NE])
        row_f = late([P, SLOTS])
        row0 = late([P, SLOTS], I32)
        multiples = late([P, NE, NT])
        over = late([P, NE, NT])
        tiles = late([P, NE])
        ends = late([P, NE])
        upto = late([P, NE, NE])
        upto_t = late([P, NE, NE])
        number = late([P, SLOTS, NE])
        passed = late([P, SLOTS, NE + 1])
        mine = late([P, SLOTS, NE])
        expert_f = late([P, SLOTS])
        expert = late([P, SLOTS], I32)
        earlier = sb("earlier", [P, P], BF16)
        ones = sb("ones", [P, P], BF16)
        blank = late([P, ROW])
        token_i = late([P, NT + 1], I32)
        wt = sb("wt", [P, X_BUFS, NE])
        weight = sb("weight", [P, X_BUFS])
        token_u = sb("token_u", [P, X_BUFS], U32)
        combT = rest[0:NE, 0, :]

        ps = ctx.enter_context(nc.psum_tensor("ps", [P, 8, BANK], F32))
        ST_BANKS, MAX_BANKS, O_BANK, MISC = (0, 1, 2), (3, 4, 5), 6, 7

        pe, dve, act, pool, sp = (Lane(sem("s_" + n)) for n in ("pe", "dve", "act", "pool", "sp"))

        def dsem(name):
            return DmaCount(sem(name))

        d_x, d_wk, d_wq, d_wv, d_misc = (dsem(n) for n in ("d_x", "d_wk", "d_wq", "d_wv", "d_misc"))
        d_blank, d_pr, d_sent, d_y0, d_add = (dsem(n) for n in ("d_blank", "d_pr", "d_sent", "d_y0", "d_add"))
        d_w1 = [dsem(f"d_w1_{r}") for r in range(W1_BUFS)]
        d_row = [dsem(f"d_row{r}") for r in range(X_BUFS)]
        d_ctx = [dsem(f"d_ctx{b}") for b in range(B)]
        cv = ctx_t.rearrange("(c p) t -> p c t", p=P)

        def w2(w):
            return w.rearrange("(c p) n -> p c n", p=P)

        got_x = sp.dma(lambda e: e.dma_start(x_sb[:, :, :], x.rearrange("(i p) e -> p i e", p=P)), d_x)
        got_wq = [act.dma(lambda e: e.dma_start(wq_sb[:, :, :], w2(wq)), d_wq),
                  act.dma(lambda e: e.dma_start(bq_sb[:, :], bq), d_wq)][-1]
        got_wk = [sp.dma(lambda e: e.dma_start(wk_sb[:, :, :], w2(wk)), d_wk),
                  sp.dma(lambda e: e.dma_start(bk_sb[:, :], bk), d_wk)][-1]
        got_ctx = [sp.dma(lambda e: e.dma_start(ctxT[:, :, 0:TB], cv[:, :, 0:TB]), d_ctx[0])]
        got_ctx.append(sp.dma(lambda e: e.dma_start(ctxT[:, :, TB:T], cv[:, :, TB:T]), d_ctx[1]))
        got_wv = sp.dma(lambda e: e.dma_start(wv_sb[:, :, :], w2(wv)), d_wv)
        for dst, src in ((wo_sb[:, :, :], w2(wo)),
                         (bv_sb[:, :], bv.partition_broadcast(P)), (bo_sb[:, :], bo.partition_broadcast(P)),
                         (router_sb[:, :, :], w2(router_t)), (b_pr_sb[:, :], b_proj)):
            got_misc = sp.dma(lambda e, d=dst, s=src: e.dma_start(d, s), d_misc)

        pool.step(lambda e: e.memset(eps_sb[:, :], EPS))
        for m in (ident, ident_b):
            pool.step(lambda e, m=m: e.memset(m[:, :], 0.0))
            made_ident = pool.step(lambda e, m=m: e.affine_select(
                out=m[:, :], in_=m[:, :], compare_op=ALU.not_equal, fill=1.0, base=0,
                pattern=[[-1, P]], channel_multiplier=1))
        pair_of_ones = float(np.array([0x3F803F80], np.uint32).view(np.float32)[0])
        made_key_ones = pool.step(lambda e: e.memset(
            k_stack[STACK:STACK + NPART, :, :, :].rearrange("p b h t -> p (b h t)").bitcast(F32), pair_of_ones))
        made_v_ones = pool.step(lambda e: e.memset(v_ones[:, :, :, D:2 * D], 1.0))

        free = {bank: [] for bank in range(8)}

        def batch_tiles(b):
            return range(b * ST, (b + 1) * ST)

        def preload(func):
            act.wait(made_ident)
            act.step(lambda e: e.activation(unused[:, :], eps_sb[:, :], func))

        def row_statistics(i, src, ready):
            dve.wait(*ready)
            dve.step(lambda e: e.bn_stats(stats[:, i, :], src[:, i, :]))
            stats_made[i] = dve.done(lambda e: e.bn_aggr(mv[:, i, :], stats[:, i, :]))

        def deviations(b):
            act.wait(*[stats_made[i] for i in batch_tiles(b)], made_ident)
            rs = rstd[:, b * ST:(b + 1) * ST]
            std = act.done(lambda e: e.activation(rs, mv[:, b * ST:(b + 1) * ST, 1], ACT.Sqrt, bias=eps_sb[:, :]))
            dve.wait(std)
            dve.step(lambda e: e.reciprocal(rs, rs))

        stats_made = {}

        def layernorm(b, src, ready):
            for i in batch_tiles(b):
                row_statistics(i, src, ready[i])
            deviations(b)
            return {i: dve.done(lambda e, i=i: e.tensor_scalar(
                xn[:, i, 0:E], src[:, i, :], mv[:, i, 0:1], rstd[:, i:i + 1], ALU.subtract, ALU.mult))
                for i in batch_tiles(b)}

        def transpose_half(b, c, ready, bank, eng):
            pe.wait(*free[bank], made_ident)
            for j, i in enumerate(batch_tiles(b)):
                pe.wait(ready[i])
                last = pe.done(lambda e, j=j, i=i: e.transpose(
                    ps[:, bank, j * P:(j + 1) * P], xn[:, i, c * P:(c + 1) * P], ident[:, :]))
            eng.wait(last)
            dst = xT[:, c, b * S:(b + 1) * S]
            if eng is act:
                t = act.done(lambda e: e.activation(dst, ps[:, bank, :], ACT.Copy))
            else:
                t = dve.done(lambda e: e.tensor_copy(dst, ps[:, bank, :]))
            free[bank] = [t]
            return t

        d_parts = [dsem("d_parts0"), dsem("d_parts1")]
        d_stack = [dsem(f"d_stack{n}") for n in range(EC * (B + 1))]
        part_rows = [nc.dram_tensor(f"part_rows{n}", [NPART, P, 1024], BF16, kind="Internal").ap()
                     for n in range(EC * (B + 1))]
        parts_read = [None, None]
        blocks = 0

        def project(w, bias, src, cols, m, ready, banks, stack, third, queue):
            nonlocal blocks
            slot = blocks
            r = slot % 2
            blocks += 1
            for n in range(2):
                pe.wait(*ready[n], *free[banks[n]])
                for c in range(EC):
                    last = pe.done(lambda e, n=n, c=c: e.matmul(
                        ps[:, banks[n], :], w[:, c, m * P:(m + 1) * P],
                        src[:, c, cols + n * BANK:cols + (n + 1) * BANK], start=c == 0, stop=c == EC - 1))
                yield 3
            block = ps[:, banks[0]:banks[0] + 2, :].rearrange("p a b -> p (a b)")
            act.wait(last)
            if parts_read[r]:
                act.wait(parts_read[r])
            p1 = act.done(lambda e: e.activation(parts[:, r, 0, :], block, ACT.Identity, bias=bias[:, m:m + 1]))
            yield 2
            dve.wait(p1)
            left = dve.done(lambda e: e.scalar_tensor_tensor(
                rest[:, r, :], block, bias[:, m:m + 1], parts[:, r, 0, :], ALU.add, ALU.subtract))
            free[banks[0]] = free[banks[1]] = [left]
            act.wait(left)
            p2 = act.done(lambda e: e.activation(parts[:, r, 1, :], rest[:, r, :], ACT.Copy))
            third.wait(p2)
            if third is pool:
                third.wait(left)
            p3 = third.step(lambda e: e.tensor_tensor(
                parts[:, r, 2, :], rest[:, r, :], parts[:, r, 1, :], ALU.subtract))
            queue.wait(p1, p2, p3)
            kept = queue.dma(lambda e: e.dma_start(
                part_rows[slot].rearrange("a (d h) t -> (d h) a t", d=D), parts[:, r, :, :]), d_parts[r])
            parts_read[r] = kept
            queue.wait(kept)
            stack(part_rows[slot].rearrange("a (d h) t -> (a d) h t", d=D), m, d_stack[slot])

        k_ready, q_ready = {}, {}

        def fill(queue, dst, src, first, m, done):
            return queue.dma(lambda e: e.dma_start(
                dst[first:first + src.shape[0], m * HPM:(m + 1) * HPM, :], src), done)

        def k_block(b, m, banks, third, queue=sp):
            def stack(src, m, done):
                for at, n in ((0, 3), (3, 2), (5, 1)):
                    k_ready[b, m] = fill(queue, k_stack[:, b, :, :], src[0:D * n], D * at, m, done)
            return project(wk_sb, bk_sb, ctxT, b * TB, m, [[got_wk, got_ctx[b]]] * 2, banks, stack, third, queue)

        def q_block(m, banks, third, queue=sp):
            def stack(src, m, done):
                for g, (part, _) in enumerate(PART_PAIRS):
                    q_ready[m] = fill(queue, q_stack, src[D * part:D * (part + 1)], D * g, m, done)
            return project(wq_sb, bq_sb, xT, 0, m, [[got_wq] + made for made in xT_made], banks, stack, third, queue)

        def v_tile(t, bank, eng):
            pe.wait(got_wv, *free[bank])
            for c in range(EC):
                last = pe.done(lambda e, c=c: e.matmul(
                    ps[:, bank, 0:E], ctxT[:, c, t * P:(t + 1) * P], wv_sb[:, c, :], start=c == 0, stop=c == EC - 1))
            eng.wait(last)
            dst, src = v_ones[:, t, :, 0:D], ps[:, bank, 0:E].rearrange("p (h d) -> p h d", h=H)
            v_made[t] = (eng.done(lambda e: e.activation(dst, src, ACT.Copy)) if eng is act
                         else eng.done(lambda e: e.tensor_copy(dst, src)))
            free[bank] = [v_made[t]]

        v_made = {}
        preload(ACT.Sqrt)
        normed = {}
        for b in range(B):
            normed.update(layernorm(b, x_sb, [[got_x]] * NT))
        xT_made = [[transpose_half(b, c, normed, 3 + 2 * b + c, act if c else dve) for c in range(EC)]
                   for b in range(B)]
        act.wait(got_wq)
        for _ in q_block(0, (0, 1), dve):
            pass
        act.wait(got_wk)
        for _ in k_block(0, 0, (2, 3), dve, act):
            pass

        def filler():
            for t in range(TT // 2):
                v_tile(t, 2 + t % 4, dve)
            for _ in k_block(0, 1, (0, 1), pool):
                pass
            yield from q_block(1, (6, 7), pool)
            yield from k_block(1, 0, (0, 1), pool)
            yield from k_block(1, 1, (6, 7), pool)
            for t in range(TT // 2, TT):
                v_tile(t, t % 3, act)
                yield 3

        groups = B * NG
        units = [(g, hh, i, n) for g in range(groups) for hh in range(HG) for i in range(ST) for n in range(TB // BANK)]
        per_group = len(units) // groups
        LEAD = per_group + 7 * per_group // 16
        emitted = 0
        neg_made, negT_ready = {}, {}
        d_neg = [dsem(f"d_neg{n}") for n in range(3)]

        def heads(g):
            return [HG * (g % NG) + hh for hh in range(HG)]

        def max_unit():
            nonlocal emitted
            g, hh, i, n = units[emitted]
            b, h = g // NG, heads(g)[hh]
            bank = MAX_BANKS[emitted % len(MAX_BANKS)]
            pe.wait(k_ready[b, h // HPM], q_ready[h // HPM], *free[bank])
            q0 = b * S + i * P
            made = pe.done(lambda e: e.matmul(ps[:, bank, :], q_stack[0:STACK, h, q0:q0 + P],
                                              k_stack[0:STACK, b, h, n * BANK:(n + 1) * BANK], start=True, stop=True))
            dve.wait(made)
            t = dve.done(lambda e: e.tensor_reduce(mx_half[:, g % 2, hh * ST + i, n:n + 1], ps[:, bank, :],
                                                   AX_X, ALU.max))
            free[bank] = [t]
            emitted += 1
            if emitted % per_group == 0:
                negate(g, t)

        def negate(g, last_max):
            r = g % 2
            nf = neg_f[:, r, :]
            dve.wait(last_max)
            dve.step(lambda e: e.tensor_reduce(nf, mx_half[:, r, :, :], AX_X, ALU.max, negate=True))
            if g >= 1:
                dve.wait(neg_transposed[g - 1])
            for part in range(NPART):
                view = neg_p[:, :, part, :].rearrange("p i h -> p h i")
                src = nf.rearrange("p (h i) -> p h i", h=HG)
                t = dve.step(lambda e, v=view, s=src: e.tensor_copy(v, s))
                if part < NPART - 1:
                    dve.step(lambda e, v=view, s=src: e.tensor_tensor(s, s, v, ALU.subtract))
            neg_made[g] = t

        neg_transposed = {}

        def spread_max(g):
            r = g % 2
            bankT = ps[0:NPART * HG, MISC, 0:S // 2].bitcast(BF16)
            pe.wait(neg_made[g], made_ident, *free[MISC])
            for i in range(ST):
                t = pe.done(lambda e, i=i: e.transpose(
                    bankT[:, i * P:(i + 1) * P], neg_p[:, i, :, :].rearrange("p a h -> p (a h)"), ident_b[:, :]))
            neg_transposed[g] = t
            act.wait(t)
            if g >= 2:
                act.wait(negT_ready[g - 2])
            moved = act.done(lambda e: e.activation(negT[:, r, :], bankT, ACT.Copy))
            free[MISC] = [moved]
            eng = sp if g else act
            eng.wait(moved)
            b = g // NG
            for hh, h in enumerate(heads(g)):
                negT_ready[g] = eng.dma(lambda e, hh=hh, h=h: e.dma_start(
                    q_stack[STACK:STACK + NPART, h, b * S:(b + 1) * S], negT[hh:NPART * HG:HG, r, :]), d_neg[1 + r if g else 0])

        exp_done = {}
        pv_done = {}
        turn = 0

        def score_heads(step, first_head, n):
            nonlocal turn
            g, j = step // KT, step % KT
            b = g // NG
            banks = ST_BANKS if emitted < len(units) else ST_BANKS + MAX_BANKS[:1]
            at = turn * n % len(banks)
            turn += 1
            pe.wait(made_key_ones, negT_ready[g], *[t for bank in banks[at:at + n] for t in free[bank]])
            for a in range(n):
                h = heads(g)[first_head + a]
                made = pe.done(lambda e, a=a, h=h: e.matmul(
                    ps[:, banks[at + a], :], k_stack[0:STACK + NPART, b, h, j * P:(j + 1) * P],
                    q_stack[0:STACK + NPART, h, b * S:(b + 1) * S], start=True, stop=True))
            act.wait(made)
            if step >= 2:
                act.wait(pv_done[step - 2])
            t = act.done(lambda e: e.activation(
                prob[:, step % 2, first_head:first_head + n, :], ps[:, banks[at]:banks[at] + n, :],
                ACT.Exp, scale=float(SCALE)))
            for bank in banks[at:at + n]:
                free[bank] = [t]
            exp_done[step] = t

        def weighted_values(step):
            g, j = step // KT, step % KT
            b = g // NG
            pe.wait(v_made[b * KT + j], made_v_ones, exp_done[step])
            if j == 0:
                pe.wait(*free[O_BANK])
            for hh, h in enumerate(heads(g)):
                t = pe.done(lambda e, hh=hh, h=h: e.matmul(
                    ps[2 * D * hh:2 * D * (hh + 1), O_BANK, :], v_ones[:, b * KT + j, h, :],
                    prob[:, step % 2, hh, :], start=j == 0, stop=j == KT - 1))
            pv_done[step] = t
            if j == KT - 1:
                act.wait(t)
                act.wait(oT_read[g - 1] if g else made_consts)
                o_moved[g] = act.done(lambda e: e.activation(oT, ps[:, O_BANK, :], ACT.Copy))
                free[O_BANK] = [o_moved[g]]

        oT_read, o_moved, attn_made = {}, {}, {}

        def normalise(g):
            b = g // NG
            pe.wait(o_moved[g], *free[MISC])
            for i in range(ST):
                t = pe.done(lambda e, i=i: e.transpose(
                    ps[:, MISC, i * P:(i + 1) * P], oT[:, i * P:(i + 1) * P], ident[:, :]))
            oT_read[g] = t
            rows = ps[:, MISC, :].rearrange("p (i h d) -> p i h d", i=ST, h=HG)
            h0 = HG * (g % NG) * D
            dst = xn[:, b * ST:(b + 1) * ST, h0:h0 + HG * D].rearrange("p i (h d) -> p i h d", h=HG)
            rs = rsum[:, :].rearrange("p (i h) -> p i h", i=ST)
            dve.wait(t)
            dve.step(lambda e: e.reciprocal(rs, rows[:, :, :, D]))
            a = dve.done(lambda e: e.tensor_tensor(
                dst, rows[:, :, :, 0:D], rs.unsqueeze(3).to_broadcast([P, ST, HG, D]), ALU.mult))
            free[MISC] = [a]
            pool.wait(got_misc, a)
            cols = xn[:, b * ST:(b + 1) * ST, h0:h0 + HG * D]
            attn_made[g] = pool.step(lambda e: e.tensor_tensor(
                cols, cols, bv_sb[:, h0:h0 + HG * D].unsqueeze(1).to_broadcast([P, ST, HG * D]), ALU.add))

        x1_made, h2_made, y_made = {}, {}, {}
        sent = None
        y_rows = out.rearrange("(i p) e -> i p e", p=P)

        def experts_of(b, t):
            return t[:, b * ST:(b + 1) * ST]

        def spread(t, n=NE):
            return t.unsqueeze(2).to_broadcast([P, ST, n])

        def after_attention(b, banks):
            nonlocal sent
            tiles_b = slice(b * ST, (b + 1) * ST)
            turned = [None, None]
            for c in range(EC):
                ready = attn_made[b * NG + (c + 1) * NG // EC - 1]
                turned[c] = transpose_half(b, c, {i: ready for i in batch_tiles(b)}, banks[c % len(banks)], act)
                yield
                for n in range(ST // 2):
                    bank = banks[n % len(banks)]
                    pe.wait(*free[bank], turned[c])
                    for a in range(2):
                        i = b * ST + 2 * n + a
                        last = pe.done(lambda e, i=i, a=a, bank=bank, c=c: e.matmul(
                            ps[:, bank, a * E:(a + 1) * E], xT[:, c, i * P:(i + 1) * P], wo_sb[:, c, :],
                            start=True, stop=True))
                    i = b * ST + 2 * n
                    dve.wait(last, x_bo, *x1_made.get(i, []))
                    t = dve.done(lambda e, i=i, bank=bank: e.tensor_tensor(
                        x_sb[:, i:i + 2, :], ps[:, bank, :].rearrange("p (a e) -> p a e", a=2),
                        x_sb[:, i:i + 2, :], ALU.add))
                    free[bank] = [t]
                    x1_made[i] = x1_made[i + 1] = [t]
                    yield
                if c == 0:
                    yield "half"
            for i in batch_tiles(b):
                row_statistics(i, x_sb, x1_made[i])
            preload(ACT.Sqrt)
            yield
            yield
            deviations(b)
            preload(ACT.Exp)
            yield
            for i in batch_tiles(b):
                h2_made[i] = dve.done(lambda e, i=i: e.tensor_scalar(
                    xn[:, i, 0:E], x_sb[:, i, :], mv[:, i, 0:1], rstd[:, i:i + 1], ALU.subtract, ALU.mult))
            yield
            yield
            for c in range(EC):
                turned[c] = transpose_half(b, c, h2_made, banks[c % len(banks)], act)
                yield
            bank = banks[0]
            pe.wait(*turned, *free[bank], got_misc)
            for i in range(ST):
                for c in range(EC):
                    last = pe.done(lambda e, i=i, c=c, bank=bank: e.matmul(
                        ps[:, bank, i * NE:(i + 1) * NE], xT[:, c, (b * ST + i) * P:(b * ST + i + 1) * P],
                        router_sb[:, c, :], start=c == 0, stop=c == EC - 1))
            lg = ps[:, bank, 0:ST * NE].rearrange("p (i e) -> p i e", i=ST)
            lb, gb, rb = logit[:, tiles_b, :], gate[:, tiles_b, :], red[:, tiles_b]
            dve.wait(last, made_consts)
            dve.step(lambda e: e.tensor_reduce(rb, lg, AX_X, ALU.max))
            t = dve.done(lambda e: e.tensor_tensor(lb, lg, spread(rb), ALU.subtract))
            free[bank] = [t]
            yield
            act.wait(t)
            t = act.done(lambda e: e.activation(gb, lb, ACT.Exp))
            if b == B - 1:
                preload(ACT.Gelu_apprx_tanh)
            yield
            dve.wait(t)
            dve.step(lambda e: e.tensor_reduce(rb, gb, AX_X, ALU.add))
            dve.step(lambda e: e.reciprocal(rb, rb))
            dve.step(lambda e: e.tensor_tensor(gb, gb, spread(rb), ALU.mult))
            for i in batch_tiles(b):
                t = dve.done(lambda e, i=i: e.max(top8[:, i, :], gate[:, i, :]))
            dve.wait(t)
            for i in batch_tiles(b):
                t = dve.done(lambda e, i=i: e.max_index(idx8[:, i, :], top8[:, i, :], gate[:, i, :]))
            dve.wait(t)
            dve.done(lambda e: e.tensor_tensor(rb, top8[:, tiles_b, 0], top8[:, tiles_b, 1], ALU.add))
            dve.step(lambda e: e.tensor_copy(idxf[:, tiles_b, :], idx8[:, tiles_b, 0:2]))
            yield
            for a in range(TOP):
                t = dve.done(lambda e, a=a: e.tensor_tensor(
                    hot[:, a, tiles_b, :], iota_e[:, :].unsqueeze(1).to_broadcast([P, ST, NE]),
                    spread(idxf[:, tiles_b, a]), ALU.is_equal))
            dve.wait(t)
            chose = dve.done(lambda e: e.tensor_tensor(
                chosen[:, tiles_b, :], hot[:, 0, tiles_b, :], hot[:, 1, tiles_b, :], ALU.add))
            bank = banks[-1]
            pe.wait(chose, made_consts, *free[bank])
            rank = ps[:, bank, 0:ST * NE].rearrange("p (i e) -> p i e", i=ST)
            total = ps[:, bank, ST * NE:(ST + 1) * NE]
            for n, i in enumerate(batch_tiles(b)):
                for k in range(b * ST, i + 1):
                    pe.done(lambda e, n=n, i=i, k=k: e.matmul(
                        rank[:, n, :], earlier[:, :] if k == i else ones[:, :], chosen[:, k, :],
                        start=k == b * ST, stop=k == i))
            for k in batch_tiles(b):
                ranked = pe.done(lambda e, k=k: e.matmul(
                    total, ones[:, :], chosen[:, k, :], start=k == b * ST, stop=k == (b + 1) * ST - 1))
            dve.step(lambda e: e.reciprocal(rb, rb))
            dve.step(lambda e: e.tensor_tensor(top8[:, tiles_b, 0:2], top8[:, tiles_b, 0:2], spread(rb, 2), ALU.mult))
            dve.wait(ranked)
            dve.done(lambda e: e.tensor_tensor(before[:, b + 1, :], before[:, b, :], total, ALU.add))
            free[bank] = [dve.step(lambda e: e.tensor_tensor(
                place[:, tiles_b, :], rank, before[:, b, :].unsqueeze(1).to_broadcast([P, ST, NE]), ALU.add))]
            for a in range(TOP):
                dve.step(lambda e, a=a: e.tensor_tensor(
                    picked[:, tiles_b, :], place[:, tiles_b, :], hot[:, a, tiles_b, :], ALU.mult))
                dve.step(lambda e, a=a: e.tensor_reduce(slot_f[:, a, tiles_b], picked[:, tiles_b, :], AX_X, ALU.add))
            slots_known = dve.done(lambda e: e.tensor_copy(slot[:, :, tiles_b], slot_f[:, :, tiles_b]))
            if b == B - 1:
                find_experts()
            for a in range(TOP):
                t = dve.done(lambda e, a=a: e.tensor_tensor(
                    hot[:, a, tiles_b, :], hot[:, a, tiles_b, :], spread(top8[:, tiles_b, a]), ALU.mult))
            dve.done(lambda e: e.memset(xn[:, tiles_b, TOKEN + 1:ROW], 0.0))
            dve.wait(t)
            dve.done(lambda e: e.tensor_copy(xn[:, tiles_b, TOKEN:TOKEN + 1], token_i[:, tiles_b].unsqueeze(2)))
            comb_made = dve.done(lambda e: e.tensor_tensor(
                xn[:, tiles_b, E:TOKEN], hot[:, 0, tiles_b, :], hot[:, 1, tiles_b, :], ALU.add))
            if b == B - 1:
                find_rows()
            pool.wait(comb_made, slots_known, blanked)
            for i in batch_tiles(b):
                for a in range(TOP):
                    sent = pool.dma(lambda e, i=i, a=a: e.indirect_dma_start(
                        out=rows_dram, out_offset=bass.IndirectOffsetOnAxis(ap=slot[:, a, i:i + 1], axis=0),
                        in_=xn[:, i, :], in_offset=None), d_sent)
            yield
            bank = banks[0]
            pe.wait(comb_made, *free[bank])
            for n, i in enumerate(batch_tiles(b)):
                last = pe.done(lambda e, n=n, i=i, bank=bank: e.transpose(
                    ps[0:NE, bank, n * P:(n + 1) * P], xn[:, i, E:TOKEN], ident[:, :]))
            act.wait(last)
            combT_made = act.done(lambda e, bank=bank: e.activation(
                combT[:, b * S:(b + 1) * S], ps[0:NE, bank, :], ACT.Copy))
            free[bank] = [combT_made]
            yield
            for n in range(ST // 2):
                bank = banks[(1 + n) % len(banks)]
                pe.wait(combT_made, *free[bank])
                for a in range(2):
                    i = b * ST + 2 * n + a
                    last = pe.done(lambda e, i=i, a=a, bank=bank: e.matmul(
                        ps[:, bank, a * E:(a + 1) * E], combT[:, i * P:(i + 1) * P], b_pr_sb[:, :],
                        start=True, stop=True))
                i = b * ST + 2 * n
                dve.wait(last)
                t = dve.done(lambda e, i=i, bank=bank: e.tensor_tensor(
                    x_sb[:, i:i + 2, :], ps[:, bank, :].rearrange("p (a e) -> p a e", a=2), x_sb[:, i:i + 2, :], ALU.add))
                free[bank] = [t]
                y_made[i] = y_made[i + 1] = t
                yield

        wide = [P, SLOTS, NE]

        def find_experts():
            nonlocal expert_known
            dve.step(lambda e: e.tensor_tensor(count[:, :], before[:, B, :], before[:, 0, :], ALU.subtract))
            dve.step(lambda e: e.tensor_tensor(over[:, :, :], count[:, :].unsqueeze(2).to_broadcast([P, NE, NT]),
                                               multiples[:, :, :], ALU.is_gt))
            dve.step(lambda e: e.tensor_reduce(tiles[:, :], over[:, :, :], AX_X, ALU.add))
            dve.step(lambda e: e.tensor_tensor(upto_t[:, :, :], upto[:, :, :],
                                               tiles[:, :].unsqueeze(1).to_broadcast([P, NE, NE]), ALU.mult))
            dve.step(lambda e: e.tensor_reduce(ends[:, :], upto_t[:, :, :], AX_X, ALU.add))
            dve.step(lambda e: e.tensor_tensor(passed[:, :, 1:NE + 1], number[:, :, :],
                                               ends[:, :].unsqueeze(1).to_broadcast(wide), ALU.is_ge))
            dve.step(lambda e: e.tensor_reduce(expert_f[:, :], passed[:, :, 1:NE + 1], AX_X, ALU.add))
            dve.step(lambda e: e.tensor_scalar(expert_f[:, :], expert_f[:, :], float(NE - 1), None, ALU.min))
            expert_known = dve.done(lambda e: e.tensor_copy(expert[:, :], expert_f[:, :]))

        def find_rows():
            nonlocal tiles_known
            dve.done(lambda e: e.tensor_tensor(mine[:, :, :], passed[:, :, 0:NE], passed[:, :, 1:NE + 1], ALU.subtract))
            dve.step(lambda e: e.tensor_tensor(first[:, :], ends[:, :], tiles[:, :], ALU.subtract))
            dve.step(lambda e: e.tensor_tensor(sel[:, :, :], mine[:, :, :],
                                               first[:, :].unsqueeze(1).to_broadcast(wide), ALU.mult))
            dve.step(lambda e: e.tensor_reduce(row_f[:, :], sel[:, :, :], AX_X, ALU.add))
            dve.step(lambda e: e.tensor_tensor(row_f[:, :], number[:, :, 0], row_f[:, :], ALU.subtract))
            dve.step(lambda e: e.tensor_scalar(row_f[:, :], row_f[:, :], float(NT - 1), float(P), ALU.min, ALU.mult))
            tiles_known = dve.step(lambda e: e.scalar_tensor_tensor(
                row0[:, :], expert_f[:, :], float(N), row_f[:, :], ALU.mult, ALU.add))

        expert_known = tiles_known = None

        for behind in filler():
            for _ in range(behind):
                if emitted < LEAD:
                    max_unit()
                    if emitted == per_group + 4:
                        spread_max(0)
        assert emitted == LEAD

        pool.wait(*k_ready.values(), *q_ready.values())
        for k in range(NE):
            pool.step(lambda e, k=k: e.memset(iota_e[:, k:k + 1], float(k)))
            pool.step(lambda e, k=k: e.memset(before[:, 0, k:k + 1], float(k * N)))
        for k in range(NT):
            pool.step(lambda e, k=k: e.memset(multiples[:, :, k:k + 1], float(P * k)))
        for j in range(SLOTS):
            pool.step(lambda e, j=j: e.memset(number[:, j, :], float(j)))
        for m in (upto, earlier, ones):
            pool.step(lambda e, m=m: e.memset(m[:, :], 1.0))
        pool.step(lambda e: e.affine_select(out=upto[:, :, :], in_=upto[:, :, :], compare_op=ALU.is_ge, fill=0.0,
                                            base=0, pattern=[[1, NE], [-1, NE]], channel_multiplier=0))
        pool.step(lambda e: e.affine_select(out=earlier[:, :], in_=earlier[:, :], compare_op=ALU.is_ge, fill=0.0,
                                            base=-1, pattern=[[1, P]], channel_multiplier=-1))
        pool.step(lambda e: e.memset(passed[:, :, 0:1], 1.0))
        pool.step(lambda e: e.memset(blank[:, :], 0.0))
        pool.step(lambda e: e.iota(token_i[:, :], pattern=[[P, NT + 1]], base=0, channel_multiplier=1))
        made_consts = pool.step(lambda e: e.tensor_copy(blank[:, TOKEN:TOKEN + 1], token_i[:, NT:NT + 1]))
        rows_dram = nc.dram_tensor("rows_dram", [NE * N, ROW], F32, kind="Internal").ap()
        pool.dma(lambda e: e.dma_start(y_rows[NT], blank[:, 0:E]), d_blank)
        blank_rows = rows_dram.rearrange("(n j p) r -> n p j r", p=P, j=NT // 4)
        pool.wait(got_misc, *normed.values())
        for i in range(NT):
            x_bo = pool.step(lambda e, i=i: e.tensor_tensor(x_sb[:, i, :], x_sb[:, i, :], bo_sb[:, :], ALU.add))

        def lay_blanks(n):
            nonlocal blanked
            blanked = pool.dma(lambda e: e.dma_start(
                blank_rows[n], blank[:, :].unsqueeze(1).to_broadcast([P, NT // 4, ROW])), d_blank)

        blanked = None
        later = iter(())
        half = None
        for step in range(groups * KT):
            g, j = step // KT, step % KT
            at_once = 1 if emitted < len(units) else 2
            for hh in range(0, HG, at_once):
                score_heads(step, hh, at_once)
                if emitted < len(units):
                    max_unit()
                if hh + at_once == (2 if at_once == 1 else HG) and step >= 1:
                    weighted_values(step - 1)
            if j == 2 and g >= 1:
                normalise(g - 1)
            elif j == 5 and g + 1 < groups:
                spread_max(g + 1)
            elif step < groups * KT - KT + 3:
                next(later, None)
            if 1 <= step < NG * KT + 1:
                pool.wait(pv_done[step - 1])
                lay_blanks(step - 1)
            if step == NG * KT + 2:
                later = after_attention(0, (MISC,))
            if step == groups * KT - KT + 3:
                for _ in later:
                    pass
                later = after_attention(1, MAX_BANKS[1:])
            if step >= groups * KT - KT + 4:
                if half is None:
                    half = next(later)
        weighted_values(groups * KT - 1)
        normalise(groups - 1)
        assert half == "half"

        for i in batch_tiles(0):
            sp.wait(y_made[i])
            sp.dma(lambda e, i=i: e.dma_start(y_rows[i], x_sb[:, i, :]), d_y0)

        pr = w_proj.rearrange("x (c p) n -> x p c n", p=P)
        for b in range(B):
            sp.wait(pv_done[(b + 1) * NG * KT - 1])
            for x_ in range(b * NE // B, (b + 1) * NE // B):
                w_pr_got = sp.dma(lambda e, x_=x_: e.dma_start(
                    w_pr_sb[:, x_ * HC * E:(x_ + 1) * HC * E].rearrange("p (c n) -> p c n", c=HC), pr[x_]), d_pr)

        for _ in later:
            pass

        turned, w1_used, rows_used, hid_used, y_sent = {}, {}, {}, {}, {}
        w1_got, row_got = {}, {}
        attention_free = [pv_done[groups * KT - 1], exp_done[groups * KT - 1]]
        sp.wait(expert_known, *attention_free)

        def fetch_first_layer(j):
            r = j % W1_BUFS
            if j >= W1_BUFS:
                sp.wait(w1_used[j - W1_BUFS])

            def start(e):
                which = e.value_load(expert[0:1, j:j + 1], min_val=0, max_val=NE - 1)
                return e.dma_start(w1_sb[r], w1[bass.ds(which, 1), :, :].rearrange("a p n -> p (a n)"))
            w1_got[j] = sp.dma(start, d_w1[r])

        def fetch_rows(j):
            x_ = j % X_BUFS
            sp.wait(sent, tiles_known)
            if j >= X_BUFS:
                sp.wait(*rows_used[j - X_BUFS])

            def start(e):
                at = e.value_load(row0[0:1, j:j + 1], min_val=0, max_val=(NE * NT - 1) * P)
                return e.dma_start(row_sb[x_], rows_dram[bass.ds(at, P), :])
            row_got[j] = sp.dma(start, d_row[x_])

        def turn_rows(j):
            x_, a = j % X_BUFS, j % 2
            tb = 6 + a
            pe.wait(row_got[j], *free[tb])
            for c in range(EC):
                t = pe.done(lambda e, c=c: e.transpose(
                    ps[:, tb, c * P:(c + 1) * P], row_sb[x_][:, c * P:(c + 1) * P], ident[:, :]))
            dve.wait(t)
            if j >= 2:
                dve.wait(w1_used[j - 2])
            turned[j] = dve.done(lambda e: e.tensor_copy(
                rowT[a], ps[:, tb, 0:E].rearrange("p (c t) -> p c t", c=EC)))
            free[tb] = [turned[j]]
            dve.wait(row_got[j])
            dve.step(lambda e: e.tensor_tensor(wt[:, x_, :], row_sb[x_][:, E:TOKEN], mine[:, j, :], ALU.mult))
            dve.step(lambda e: e.tensor_reduce(weight[:, x_:x_ + 1], wt[:, x_, :], AX_X, ALU.add))
            if j >= X_BUFS:
                dve.wait(y_sent[j - X_BUFS])
            numbered = dve.done(lambda e: e.tensor_copy(token_u[:, x_:x_ + 1], row_sb[x_][:, TOKEN:TOKEN + 1]))
            rows_used[j] = [t, numbered]

        def first_layer(j):
            r, a = j % W1_BUFS, j % 2
            pe.do(lambda e: second.update({j: e.value_load(
                expert[0:1, j:j + 1], min_val=0, max_val=NE - 1) * (HC * E)}))
            pe.wait(turned[j], w1_got[j])
            w1v = w1_sb[r][:, 0:EC * HID].rearrange("p (c h) -> p c h", c=EC)
            if j >= 2:
                act.wait(hid_used[j - 2])
            for n in range(2):
                bank = 2 * a + n
                pe.wait(*free[bank])
                for q in range(HC // 2):
                    c2 = n * (HC // 2) + q
                    for c in range(EC):
                        last = pe.done(lambda e, q=q, c2=c2, c=c, bank=bank: e.matmul(
                            ps[:, bank, q * P:(q + 1) * P], w1v[:, c, c2 * P:(c2 + 1) * P], rowT[a][:, c, :],
                            start=c == 0, stop=c == EC - 1))
                act.wait(last)
                for q in range(HC // 2):
                    c2 = n * (HC // 2) + q
                    t = act.done(lambda e, q=q, c2=c2, bank=bank: e.activation(
                        hidT[a][:, c2, :], ps[:, bank, q * P:(q + 1) * P], ACT.Gelu_apprx_tanh,
                        bias=w1_sb[r][:, EC * HID + c2:EC * HID + c2 + 1]))
                free[bank] = [t]
            w1_used[j] = t
            return t

        def second_layer(j, made):
            a = j % 2
            bank = 4 + a
            pe.wait(made, w_pr_got, *free[bank])
            for c2 in range(HC):
                last = pe.done(lambda e, c2=c2: e.matmul(
                    ps[:, bank, 0:E], hidT[a][:, c2, :],
                    w_pr_sb[:, bass.ds(second[j] + c2 * E, E)], start=c2 == 0, stop=c2 == HC - 1))
            hid_used[j] = last
            dve.wait(last)
            if j >= 2:
                dve.wait(y_sent[j - 2])
            scaled = dve.done(lambda e: e.tensor_scalar(
                y_sb[a], ps[:, bank, 0:E], weight[:, j % X_BUFS:j % X_BUFS + 1], None, ALU.mult))
            free[bank] = [scaled]
            pool.wait(scaled, y_kept, blanked)
            if j >= 1:
                pool.wait(y_sent[j - 1])
            y_sent[j] = pool.dma(lambda e: e.indirect_dma_start(
                out=out, out_offset=bass.IndirectOffsetOnAxis(ap=token_u[:, j % X_BUFS:j % X_BUFS + 1], axis=0),
                in_=y_sb[a], in_offset=None, compute_op=ALU.add), d_add)

        hid_made, second = {}, {}
        pe.wait(expert_known)
        fetch_first_layer(0)
        for j in range(2):
            fetch_rows(j)
        fetch_first_layer(1)
        for i in batch_tiles(1):
            sp.wait(y_made[i])
            y_kept = sp.dma(lambda e, i=i: e.dma_start(y_rows[i], x_sb[:, i, :]), d_y0)
        fetch_first_layer(2)
        turn_rows(0)
        for j in range(SLOTS):
            hid_made[j] = first_layer(j)
            if j + W1_BUFS < SLOTS:
                fetch_first_layer(j + W1_BUFS)
            if j + 1 < SLOTS:
                turn_rows(j + 1)
            if j >= 1:
                second_layer(j - 1, hid_made[j - 1])
            if j + 2 < SLOTS:
                fetch_rows(j + 2)
        second_layer(SLOTS - 1, hid_made[SLOTS - 1])
        pool.wait(y_sent[SLOTS - 1])
        sp.wait(y_kept, blanked, y_sent[SLOTS - 1])

        block = ctx.enter_context(nc.Block())
        block.sync(lambda e: sp.emit(e))
        block.gpsimd(lambda e: pool.emit(e))
        block.scalar(lambda e: act.emit(e))
        block.vector(lambda e: dve.emit(e))
        block.tensor(lambda e: pe.emit(e))


def kernel(x, ctx_1024, L0_xattn_Wq, L0_xattn_bq, L0_xattn_Wk, L0_xattn_bk, L0_xattn_Wv, L0_xattn_bv,
           L0_xattn_Wo, L0_xattn_bo, L0_ffn_router_w, L0_ffn_w_fc, L0_ffn_b_fc, L0_ffn_w_proj, L0_ffn_b_proj):
    import concourse.bacc as bacc
    from concourse.bass_utils import run_bass_kernel_spmd

    def columns(w):
        w = np.asarray(w)
        return w.transpose(1, 0, 2).reshape(w.shape[1], -1)

    x = np.asarray(x)
    w_fc, b_fc = np.asarray(L0_ffn_w_fc), np.asarray(L0_ffn_b_fc)
    n_exp, n_feat, n_hid = w_fc.shape
    w1 = np.concatenate([
        w_fc.reshape(n_exp, n_feat // P, P, n_hid).transpose(0, 2, 1, 3).reshape(n_exp, P, -1),
        b_fc.reshape(n_exp, -1, P).transpose(0, 2, 1)], axis=2)
    def by_dim(w):
        w = np.asarray(w)
        return w.reshape(2, 8, -1, w.shape[-1]).transpose(2, 0, 3, 1)

    arrays = {
        "x": x.reshape(-1, x.shape[-1]),
        "ctx_t": np.asarray(ctx_1024).reshape(-1, x.shape[-1]).T,
        "wq": by_dim(L0_xattn_Wq).reshape(x.shape[-1], -1), "bq": by_dim(L0_xattn_bq).reshape(2, P).T,
        "wk": by_dim(L0_xattn_Wk).reshape(x.shape[-1], -1), "bk": by_dim(L0_xattn_bk).reshape(2, P).T,
        "wv": columns(L0_xattn_Wv), "bv": np.asarray(L0_xattn_bv).reshape(-1),
        "wo": np.asarray(L0_xattn_Wo), "bo": np.asarray(L0_xattn_bo),
        "router_t": np.asarray(L0_ffn_router_w).T,
        "w1": w1,
        "w_proj": np.asarray(L0_ffn_w_proj), "b_proj": np.asarray(L0_ffn_b_proj),
    }
    arrays = {f"in_{k}": np.ascontiguousarray(v) for k, v in arrays.items()}
    nc = bacc.Bacc("TRN2", target_bir_lowering=False, num_devices=1)
    ins = [nc.dram_tensor(k, v.shape, mybir.dt.from_np(v.dtype), kind="ExternalInput").ap() for k, v in arrays.items()]
    tokens, features = arrays["in_x"].shape
    out = nc.dram_tensor("out_y", (tokens + P, features), F32, kind="ExternalOutput").ap()
    xattn_moe_block(nc, *ins, out)
    r = run_bass_kernel_spmd(nc, [arrays], core_ids=[0])
    return r.results[0]["out_y"][:tokens].reshape(x.shape)
```
